# Optimizing a Trainium2 kernel written in Bass

```python
import numpy as np
import jax
import jax.numpy as jnp

def _softmax(x, axis=-1):
    return jax.nn.softmax(x, axis=axis)

def _gelu(x):
    return jax.nn.gelu(x, approximate=True)

def _silu(x):
    return jax.nn.silu(x)

def _sigmoid(x):
    return jax.nn.sigmoid(x)

def _layernorm(x, axis=-1, eps=1e-05):
    m = jnp.mean(x, axis=axis, keepdims=True)
    v = jnp.var(x, axis=axis, keepdims=True)
    return (x - m) / jnp.sqrt(v + eps)

def _scatter_add(tgt, idx, src, axis=0):
    return tgt.at[idx].add(src)

def _segment_sum(src, seg, n):
    return jax.ops.segment_sum(src, seg, n)
kernel_name = 'mk_xattn_ffn_d1_seqx_r4_dd53a2'

def setup_inputs(seed: int=0):
    np.random.seed(seed)
    _w = jnp.asarray

    def _rec_inputs():
        import jax
        import jax.numpy as jnp
        _rk = jax.random.key(seed)
        x = -0.0005207 + 1.001 * jax.random.normal(jax.random.fold_in(_rk, 1), (16, 100, 256), jnp.float32)
        _lenS = 100 - jax.random.randint(jax.random.fold_in(_rk, 7), (16,), 0, max(1, 100 // 4) + 1, jnp.int32)
        _lenS2 = 361 - jax.random.randint(jax.random.fold_in(_rk, 8), (16,), 0, max(1, 361 // 4) + 1, jnp.int32)
        _ctx_1024P = jax.random.normal(jax.random.fold_in(_rk, 11), (16, 16, 256), jnp.float32)
        _ctx_1024c = jax.random.dirichlet(jax.random.fold_in(_rk, 511), 0.3 * jnp.ones((16,), jnp.float32), (16, 361))
        _ctx_1024t = jnp.einsum('bsk,bkd->bsd', _ctx_1024c, _ctx_1024P)
        _ctx_1024t = _ctx_1024t * jax.lax.rsqrt(jnp.mean(jnp.square(_ctx_1024t)) + 1e-12) * 0.953939
        ctx_1024 = -0.000514642 + 1.00011 * (_ctx_1024t + 0.3 * jax.random.normal(jax.random.fold_in(_rk, 611), (16, 361, 256), jnp.float32))
        return (x, ctx_1024)
    x, ctx_1024 = _rec_inputs()

    def _L0_xattn_setup():
        import jax, jax.numpy as jnp
        import numpy as np
        EMBED_DIM = 256
        NUM_HEADS = 16
        HEAD_DIM = EMBED_DIM // NUM_HEADS
        WINDOW = 64

        def apply_rope(x):
            B, H, S, d = x.shape
            half = d // 2
            pos = jnp.arange(S, dtype=x.dtype)
            freqs = 1.0 / 10000.0 ** (jnp.arange(half, dtype=x.dtype) / half)
            ang = pos[:, None] * freqs[None, :]
            cos, sin = (jnp.cos(ang), jnp.sin(ang))
            x1, x2 = (x[..., :half], x[..., half:])
            return jnp.concatenate([x1 * cos - x2 * sin, x1 * sin + x2 * cos], axis=-1)

        def _forward(query, key, value, q_w, q_b, k_w, k_b, v_w, v_b, o_w, o_b):
            B, S_q, D = query.shape
            S_k = key.shape[1]
            H, d, W = (NUM_HEADS, HEAD_DIM, WINDOW)
            q = (query @ q_w.T + q_b).reshape(B, S_q, H, d).transpose(0, 2, 1, 3)
            k = (key @ k_w.T + k_b).reshape(B, S_k, H, d).transpose(0, 2, 1, 3)
            v = (value @ v_w.T + v_b).reshape(B, S_k, H, d).transpose(0, 2, 1, 3)
            q = apply_rope(q) * d ** (-0.5)
            k = apply_rope(k)
            q_pos = jnp.arange(S_q)[:, None]
            offsets = jnp.arange(-W, 1)[None, :]
            idx = q_pos + offsets
            local_mask = (idx < 0) | (idx >= S_k)
            gidx = jnp.clip(idx, 0, S_k - 1)
            k_win = k[:, :, gidx, :]
            v_win = v[:, :, gidx, :]
            scores = jnp.einsum('bhqd,bhqwd->bhqw', q, k_win)
            mask = local_mask[None, None, :, :]
            scores = jnp.where(mask, -jnp.inf, scores)
            m = jnp.max(scores, axis=-1, keepdims=True)
            m = jnp.where(jnp.isfinite(m), m, 0.0)
            e = jnp.exp(scores - m)
            denom = jnp.sum(e, axis=-1, keepdims=True)
            probs = jnp.where(denom > 0, e / jnp.where(denom > 0, denom, 1.0), 0.0)
            ctx = jnp.einsum('bhqw,bhqwd->bhqd', probs, v_win)
            ctx = ctx.transpose(0, 2, 1, 3).reshape(B, S_q, D)
            return ctx @ o_w.T + o_b
        key = jax.random.key(seed)
        ks = jax.random.split(key, 12)
        B, S, D = (1, 512, EMBED_DIM)
        scale = 1.0 / np.sqrt(D)
        inp = {'query': jax.random.normal(ks[0], (B, S, D), jnp.float32), 'key': jax.random.normal(ks[1], (B, S, D), jnp.float32), 'value': jax.random.normal(ks[2], (B, S, D), jnp.float32), 'q_w': jax.random.normal(ks[3], (D, D), jnp.float32) * scale, 'q_b': jax.random.normal(ks[4], (D,), jnp.float32) * 0.01, 'k_w': jax.random.normal(ks[5], (D, D), jnp.float32) * scale, 'k_b': jax.random.normal(ks[6], (D,), jnp.float32) * 0.01, 'v_w': jax.random.normal(ks[7], (D, D), jnp.float32) * scale, 'v_b': jax.random.normal(ks[8], (D,), jnp.float32) * 0.01, 'o_w': jax.random.normal(ks[9], (D, D), jnp.float32) * scale, 'o_b': jax.random.normal(ks[10], (D,), jnp.float32) * 0.01}
        return inp
    _L0_xattn_all = _L0_xattn_setup()
    _L0_xattn_in = {k: v for k, v in _L0_xattn_all.items() if k in ('q_w', 'q_b', 'k_w', 'k_b', 'v_w', 'v_b', 'o_w', 'o_b')}
    del _L0_xattn_all

    def _L0_ffn_setup():
        import jax, jax.numpy as jnp
        import numpy as np
        TOP_K = 2
        key = jax.random.key(seed)
        ks = jax.random.split(key, 5)
        B, S, H, I, E = (4, 512, 256, 1024, 8)
        scale_hi = (2.0 / (H + I)) ** 0.5
        scale_he = (2.0 / (H + E)) ** 0.5
        return {'x': jax.random.normal(ks[0], (B, S, H), dtype=jnp.float32), 'router_w': jax.random.normal(ks[1], (E, H), dtype=jnp.float32) * scale_he, 'gate_w': jax.random.normal(ks[2], (E, I, H), dtype=jnp.float32) * scale_hi, 'up_w': jax.random.normal(ks[3], (E, I, H), dtype=jnp.float32) * scale_hi, 'down_w': jax.random.normal(ks[4], (E, H, I), dtype=jnp.float32) * scale_hi}
    _L0_ffn_all = _L0_ffn_setup()
    _L0_ffn_in = {k: v for k, v in _L0_ffn_all.items() if k in ('router_w', 'gate_w', 'up_w', 'down_w')}
    del _L0_ffn_all
    return {'x': x, 'ctx_1024': ctx_1024, 'L0_xattn_q_w': _L0_xattn_in['q_w'], 'L0_xattn_q_b': _L0_xattn_in['q_b'], 'L0_xattn_k_w': _L0_xattn_in['k_w'], 'L0_xattn_k_b': _L0_xattn_in['k_b'], 'L0_xattn_v_w': _L0_xattn_in['v_w'], 'L0_xattn_v_b': _L0_xattn_in['v_b'], 'L0_xattn_o_w': _L0_xattn_in['o_w'], 'L0_xattn_o_b': _L0_xattn_in['o_b'], 'L0_ffn_router_w': _L0_ffn_in['router_w'], 'L0_ffn_gate_w': _L0_ffn_in['gate_w'], 'L0_ffn_up_w': _L0_ffn_in['up_w'], 'L0_ffn_down_w': _L0_ffn_in['down_w']}

def reference(x, ctx_1024, L0_xattn_q_w, L0_xattn_q_b, L0_xattn_k_w, L0_xattn_k_b, L0_xattn_v_w, L0_xattn_v_b, L0_xattn_o_w, L0_xattn_o_b, L0_ffn_router_w, L0_ffn_gate_w, L0_ffn_up_w, L0_ffn_down_w):
    import jax
    import jax.numpy as jnp

    def _L0_xattn_ref(query, key, value, q_w, q_b, k_w, k_b, v_w, v_b, o_w, o_b):
        import jax, jax.numpy as jnp
        import numpy as np
        EMBED_DIM = 256
        NUM_HEADS = 16
        HEAD_DIM = EMBED_DIM // NUM_HEADS
        WINDOW = 64

        def apply_rope(x):
            B, H, S, d = x.shape
            half = d // 2
            pos = jnp.arange(S, dtype=x.dtype)
            freqs = 1.0 / 10000.0 ** (jnp.arange(half, dtype=x.dtype) / half)
            ang = pos[:, None] * freqs[None, :]
            cos, sin = (jnp.cos(ang), jnp.sin(ang))
            x1, x2 = (x[..., :half], x[..., half:])
            return jnp.concatenate([x1 * cos - x2 * sin, x1 * sin + x2 * cos], axis=-1)

        def _forward(query, key, value, q_w, q_b, k_w, k_b, v_w, v_b, o_w, o_b):
            B, S_q, D = query.shape
            S_k = key.shape[1]
            H, d, W = (NUM_HEADS, HEAD_DIM, WINDOW)
            q = (query @ q_w.T + q_b).reshape(B, S_q, H, d).transpose(0, 2, 1, 3)
            k = (key @ k_w.T + k_b).reshape(B, S_k, H, d).transpose(0, 2, 1, 3)
            v = (value @ v_w.T + v_b).reshape(B, S_k, H, d).transpose(0, 2, 1, 3)
            q = apply_rope(q) * d ** (-0.5)
            k = apply_rope(k)
            q_pos = jnp.arange(S_q)[:, None]
            offsets = jnp.arange(-W, 1)[None, :]
            idx = q_pos + offsets
            local_mask = (idx < 0) | (idx >= S_k)
            gidx = jnp.clip(idx, 0, S_k - 1)
            k_win = k[:, :, gidx, :]
            v_win = v[:, :, gidx, :]
            scores = jnp.einsum('bhqd,bhqwd->bhqw', q, k_win)
            mask = local_mask[None, None, :, :]
            scores = jnp.where(mask, -jnp.inf, scores)
            m = jnp.max(scores, axis=-1, keepdims=True)
            m = jnp.where(jnp.isfinite(m), m, 0.0)
            e = jnp.exp(scores - m)
            denom = jnp.sum(e, axis=-1, keepdims=True)
            probs = jnp.where(denom > 0, e / jnp.where(denom > 0, denom, 1.0), 0.0)
            ctx = jnp.einsum('bhqw,bhqwd->bhqd', probs, v_win)
            ctx = ctx.transpose(0, 2, 1, 3).reshape(B, S_q, D)
            return ctx @ o_w.T + o_b
        return _forward(query, key, value, q_w, q_b, k_w, k_b, v_w, v_b, o_w, o_b)

    def _L0_ffn_ref(x, router_w, gate_w, up_w, down_w):
        import jax, jax.numpy as jnp
        import numpy as np
        TOP_K = 2
        B, S, H = x.shape
        E = router_w.shape[0]
        xf = x.reshape(-1, H)
        logits = xf @ router_w.T
        probs = jax.nn.softmax(logits, axis=-1)
        topk_p, topk_i = jax.lax.top_k(probs, TOP_K)
        topk_p = topk_p / topk_p.sum(axis=-1, keepdims=True)

        def body(out, inputs):
            e, gw, uw, dw = inputs
            sel = topk_i == e
            mask = sel.any(axis=-1)
            w_tok = (topk_p * sel).sum(axis=-1)
            cnt = mask.sum().astype(xf.dtype)
            mean_w = jnp.where(cnt > 0, w_tok.sum() / jnp.maximum(cnt, 1.0), 0.0)
            h = jax.nn.silu(xf @ gw.T) * (xf @ uw.T)
            eo = h @ dw.T
            out = out + mask[:, None].astype(xf.dtype) * eo * mean_w
            return (out, None)
        out0 = jnp.zeros_like(xf)
        out, _ = jax.lax.scan(body, out0, (jnp.arange(E), gate_w, up_w, down_w))
        return out.reshape(B, S, H)
    x = x + _L0_xattn_ref(_layernorm(x, axis=-1), ctx_1024, ctx_1024, L0_xattn_q_w, L0_xattn_q_b, L0_xattn_k_w, L0_xattn_k_b, L0_xattn_v_w, L0_xattn_v_b, L0_xattn_o_w, L0_xattn_o_b)
    x = x + _L0_ffn_ref(_layernorm(x, axis=-1), L0_ffn_router_w, L0_ffn_gate_w, L0_ffn_up_w, L0_ffn_down_w)
    return x

_drawn_inputs = setup_inputs


def setup_inputs(seed=0):
    import zlib

    import numpy as np

    out = dict(_drawn_inputs(seed))
    spreads = {}
    factors = {'L0_xattn_q_b': 8.0, 'L0_xattn_k_b': 22.411, 'L0_xattn_v_b': 2.942, 'L0_xattn_o_b': 4.195}
    for name, (base, spread) in spreads.items():
        noise = np.random.default_rng([zlib.crc32(name.encode()), seed]).standard_normal(out[name].shape)
        drawn = base * np.exp(spread * noise) if base else spread * noise
        out[name] = jnp.asarray(drawn.astype(out[name].dtype))
    for name, factor in factors.items():
        out[name] = (out[name] * factor).astype(out[name].dtype)
    return out
```

```python
from contextlib import ExitStack

import numpy as np

import concourse.bass as bass
from concourse import mybir

F32 = mybir.dt.float32
BF16 = mybir.dt.bfloat16
I32 = mybir.dt.int32
U32 = mybir.dt.uint32
ALU = mybir.AluOpType
ACT = mybir.ActivationFunctionType
AX = mybir.AxisListType

B, S, D = 16, 100, 256
H, DH, WINDOW = 16, 16, 64
E, FF, TOPK = 8, 1024, 2
EPS = 1e-5
TOK = B * S
P = 128
DC = D // P
HC = H // DC
FC = FF // P
NPAIR = B // 2
PT = 2 * S
QH = 4
NQ = 2 * H // QH
TILE = 128
MAXT = -(-TOK // TILE)
REGION = MAXT * TILE + TILE
RW = D + 1
MAXTILES = TOPK * TOK // TILE + E
NEG = -1e30
HF = FC // 2

C_ID, C_TRI, C_ONE, C_MASK = 0, 128, 256, 384
C_ROPE = C_MASK + S
C_PAR = C_ROPE + 4 * S
C_EXP = C_PAR + 2
C_BASE = C_EXP + E
C_TAIL = C_BASE + E
C_THR = C_TAIL + E
C_LT = C_THR + E * (MAXT - 1)
C_ALL = C_LT + (E + 1) * E


def shape_constants():
    c = np.zeros((P, C_ALL), np.float32)
    p = np.arange(P)
    c[:, C_ID:C_ID + P] = np.eye(P)
    c[:, C_TRI:C_TRI + P] = p[:, None] < p[None, :]
    c[:, C_ONE:C_ONE + P] = 1
    k = np.arange(S)
    seen = (k[None, :] <= p[:, None]) & (k[None, :] >= p[:, None] - WINDOW)
    c[:, C_MASK:C_MASK + S] = np.where(seen, 0, NEG)
    half = DH // 2
    freqs = np.float32(1) / np.float32(10000) ** (np.arange(half, dtype=np.float32) / np.float32(half))
    ang = (np.arange(S, dtype=np.float32)[:, None] * freqs[None, :]).astype(np.float32)
    j = p % half
    cos, sin = np.cos(ang).T[j], np.sin(ang).T[j] * np.where(p % DH < half, -1, 1)[:, None]
    for n, (t, scale) in enumerate(((cos, DH ** -0.5), (sin, DH ** -0.5), (cos, 1), (sin, 1))):
        c[:, C_ROPE + n * S:C_ROPE + (n + 1) * S] = t * scale
    c[:, C_PAR] = p // DH % 2 == 0
    c[:, C_PAR + 1] = p // DH % 2 == 1
    c[:, C_EXP:C_EXP + E] = np.arange(E)
    c[:, C_BASE:C_BASE + E] = np.arange(E) * REGION
    c[:, C_TAIL:C_TAIL + E] = np.arange(E) * REGION + p[:, None]
    c[:, C_THR:C_LT] = np.tile(TILE * np.arange(1, MAXT), E)
    c[:, C_LT:C_ALL] = (np.arange(E)[None, :] < np.arange(E + 1)[:, None]).ravel()
    rows = np.zeros((P, B + 1), np.int32)
    rows[:, :B] = np.arange(B)[None, :] * S + p[:, None]
    rows[:, B] = TOK + p
    return c, rows


def build(nc, x, ctxT, wT, bT, brow, rwT, ffw, consts, rownum, out):
    ctx = ExitStack()
    with ctx:
        def sb(name, shape, dt=F32):
            return ctx.enter_context(nc.sbuf_tensor(name, shape, dt))

        def bank(name):
            return ctx.enter_context(nc.psum_tensor(name, [P, 512], F32))

        def sem(name):
            return ctx.enter_context(nc.semaphore(name))

        slots = nc.dram_tensor("slots", (E * REGION, RW), F32, kind="Internal").ap()

        cst = sb("cst", [P, C_ALL])
        rows_sb = sb("rows_sb", [P, B + 1], I32)
        ident = cst[:, C_ID:C_ID + P]
        ident_bf = sb("ident_bf", [P, P], BF16)
        tri_bf = sb("tri_bf", [P, P], BF16)
        ones_bf = sb("ones_bf", [P, P], BF16)
        mask_bf = sb("mask_bf", [P, QH, S], BF16)
        attw = sb("attw", [P, 4, DC, D])
        attb = sb("attb", [P, 2, DC])
        biasrow = sb("biasrow", [S, 2, D])
        rw_sb = sb("rw_sb", [P, DC, E])
        eps_exp = sb("eps_exp", [P, 2])
        x_all = sb("x_all", [S, B, D])
        ctx_all = sb("ctx_all", [P, DC, TOK])
        stats = sb("stats", [S, 2, 6])
        mv = sb("mv", [S, 2, 2])
        ve = sb("ve", [S, 2])
        rstd = sb("rstd", [S, 2])
        xn = sb("xn", [S, 2, D])
        xnT = sb("xnT", [P, DC, PT])
        proj = sb("proj", [P, 2, DC * 2, S])
        swap = sb("swap", [P, 2, DC * 2, S])
        krot = sb("krot", [P, DC * 2, S])
        qrot = sb("qrot", [P, 2, DC * 2, S])
        kblk = sb("kblk", [P, 2, DC, HC, PT])
        v_sb = sb("v_sb", [S, 2, 2, D])
        negmax = sb("negmax", [S, 4, QH])
        probs = sb("probs", [S, 3, QH, S])
        psums = sb("psums", [S, 2, H])
        rden = sb("rden", [S, 2, H])
        rdenx = sb("rdenx", [S, H, DH])
        probsT = sb("probsT", [S, 2, QH, S])
        rdenT = sb("rdenT", [P, DC, S])
        ev0 = sb("ev0", [P, DC, S])
        ev1 = sb("ev1", [P, DC, S])
        att = sb("att", [P, 2, DC, S])
        stats2 = sb("stats2", [S, 2, 6])
        mv2 = sb("mv2", [S, 2, 2])
        ve2 = sb("ve2", [S, 2])
        rstd2 = sb("rstd2", [S, 2])
        xrow = sb("xrow", [S, 2, 2, RW])
        xn2T = sb("xn2T", [P, 2, DC, S])
        logits = sb("logits", [S, 2, E])
        top = sb("top", [S, NPAIR, 2, E])
        topi = sb("topi", [S, 2, E], U32)
        choice = sb("choice", [S, TOPK, 2])
        sel = sb("sel", [S, NPAIR, TOPK * 2, E])
        delta = sb("delta", [S, TOPK, B])
        etop = sb("etop", [S, TOPK, B])
        esum = sb("esum", [S, B])
        erec = sb("erec", [S, B])
        wtop = sb("wtop", [S, TOPK, B])
        wsel = sb("wsel", [S, NPAIR, TOPK * 2, E])
        chosen = sb("chosen", [S, 2, E], BF16)
        before = sb("before", [S, 3, E], BF16)
        place = sb("place", [S, 2, E])
        placed = sb("placed", [S, TOPK * 2, E])
        dest = sb("dest", [S, TOPK * 2])
        desti = sb("desti", [S, 2, TOPK * 2], U32)
        wacc = sb("wacc", [S, E])
        credit = sb("credit", [1, 8])
        cnt = sb("cnt", [P, E])
        cnt1 = sb("cnt1", [P, E])
        crec = sb("crec", [P, E])
        meanw = sb("meanw", [P, E])
        taili = sb("taili", [P, E], U32)
        tailrow = sb("tailrow", [P, RW])
        over = sb("over", [1, E, MAXT - 1])
        ntile = sb("ntile", [1, E])
        ntile1 = sb("ntile1", [1, E])
        upto = sb("upto", [1, E + 1, E])
        first_f = sb("first_f", [1, E + 1])
        first = sb("first", [1, E + 1], I32)
        wbuf = sb("wbuf", [P, 2, 3 * DC * FF])
        xin = sb("xin", [TILE, RW])
        idnext = sb("idnext", [TILE, 1], I32)
        idnow = sb("idnow", [TILE, 1], I32)
        xT = sb("xT", [P, DC, TILE])
        act = sb("act", [P, 2, HF, TILE])
        hT = sb("hT", [P, FC, TILE])
        y_sb = sb("y_sb", [TILE, D])

        b_small = bank("b_small")
        b_proj = bank("b_proj")
        b_o = bank("b_o")
        b_s = [bank(f"b_s{n}") for n in range(3)]
        b_pt = bank("b_pt")
        b_pv = bank("b_pv")
        b_gate = [b_s[0], b_s[1]]
        b_up = [b_s[2], b_pt]
        b_y = b_pv
        b_xt = b_proj

        wq, wk, wv, wo = (attw[:, n] for n in range(4))

        def wpart(par):
            w = wbuf[:, par]
            n = DC * FF
            return (w[:, 0:n].rearrange("p (c f) -> p c f", c=DC),
                    w[:, n:2 * n].rearrange("p (c f) -> p c f", c=DC),
                    w[:, 2 * n:3 * n].rearrange("p (f d) -> p f d", d=D))

        s_cst = sem("s_cst")
        s_wk = sem("s_wk")
        s_w = sem("s_w")
        s_x = [sem(f"s_x{i}") for i in range(2)]
        s_ctx = [sem(f"s_ctx{i}") for i in range(2)]
        s_setup = sem("s_setup")
        s_zero = sem("s_zero")
        dve = sem("dve")
        pool_self = sem("pool_self")
        s_var = sem("s_var")
        s_rstd = sem("s_rstd")
        s_xn = sem("s_xn")
        s_xnT = sem("s_xnT")
        s_xnTc = sem("s_xnTc")
        s_k = sem("s_k")
        s_kc = sem("s_kc")
        s_q = sem("s_q")
        s_qc = sem("s_qc")
        s_v = sem("s_v")
        s_vc = sem("s_vc")
        s_krot = sem("s_krot")
        s_kblk = sem("s_kblk")
        s_qrot = sem("s_qrot")
        s_s = sem("s_s")
        s_max = sem("s_max")
        s_p = sem("s_p")
        s_pT = sem("s_pT")
        s_pTc = sem("s_pTc")
        s_pv = sem("s_pv")
        s_rx = sem("s_rx")
        s_rT = sem("s_rT")
        s_rTc = sem("s_rTc")
        s_att = sem("s_att")
        s_o = sem("s_o")
        s_xob = sem("s_xob")
        s_x2 = sem("s_x2")
        s_out = sem("s_out")
        s_var2 = sem("s_var2")
        s_rstd2 = sem("s_rstd2")
        s_xr = sem("s_xr")
        s_x2T = sem("s_x2T")
        s_x2Tc = sem("s_x2Tc")
        s_lg = sem("s_lg")
        s_lgc = sem("s_lgc")
        s_dl = sem("s_dl")
        s_et = sem("s_et")
        s_ch = sem("s_ch")
        s_rk = sem("s_rk")
        s_rkc = sem("s_rkc")
        s_dest = sem("s_dest")
        s_scat = [sem(f"s_scat{i}") for i in range(2)]
        s_wacc = sem("s_wacc")
        s_cnt = sem("s_cnt")
        s_wsum = sem("s_wsum")
        s_tail = sem("s_tail")
        s_tails = [sem(f"s_tails{e}") for e in range(E)]
        s_first = sem("s_first")
        s_ew = [sem(f"s_ew{i}") for i in range(2)]
        s_in = sem("s_in")
        s_xt = sem("s_xt")
        s_xtc = sem("s_xtc")
        s_id = sem("s_id")
        s_gate = sem("s_gate")
        s_up = sem("s_up")
        s_act = sem("s_act")
        s_h = sem("s_h")
        s_down = sem("s_down")
        s_y = sem("s_y")
        s_add = sem("s_add")
        s_idnow = sem("s_idnow")

        block = ctx.enter_context(nc.Block())
        pairs = range(NPAIR)

        def tokens(i):
            return slice(i * PT, (i + 1) * PT)

        @block.sync
        def _(sp):
            sp.dma_start(cst[:, :], consts).then_inc(s_cst, 16)
            sp.dma_start(x_all[:, 0:2, :], x[0:2].rearrange("b s d -> s b d")).then_inc(s_x[0], 16)
            sp.dma_start(ctx_all[:, :, tokens(0)], ctxT[:, :, tokens(0)]).then_inc(s_ctx[0], 16)
            sp.dma_start(x_all[:, 2:B, :], x[2:B].rearrange("b s d -> s b d")).then_inc(s_x[1], 16)
            sp.dma_start(ctx_all[:, :, PT:TOK], ctxT[:, :, PT:TOK]).then_inc(s_ctx[1], 16)
            sp.wait_ge(s_zero, 2)
            sp.dma_start(out[TOK:TOK + P, :], tailrow[:, 0:D]).then_inc(s_out, 16)

            def key_blocks(i):
                sp.wait_ge(s_krot, i + 1)
                if i >= 2:
                    sp.wait_ge(s_s, NQ * (i - 1))
                for c in range(DC):
                    for h in range(HC):
                        r = slice(h * DH, (h + 1) * DH)
                        sp.dma_start(kblk[r, i % 2, c, h, :],
                                     krot[r, 2 * c:2 * c + 2, :].rearrange("p b s -> p (b s)")
                                     ).then_inc(s_kblk, 16)

            def store_x2(i):
                sp.wait_ge(s_x2, i + 1)
                sp.dma_start(out[tokens(i), :].rearrange("(b s) d -> s b d", b=2),
                             x_all[:, 2 * i:2 * i + 2, :]).then_inc(s_out, 16)

            sp.wait_ge(s_zero, 3)
            key_blocks(0)
            for i in pairs:
                if i + 1 < NPAIR:
                    key_blocks(i + 1)
                if i >= 1:
                    store_x2(i - 1)
            store_x2(NPAIR - 1)

            sp.wait_ge(s_first, 1)
            for q in s_scat:
                sp.wait_ge(q, 16 * TOPK * 2 * (NPAIR // 2))
            for e in range(E):
                lo = sp.value_load(first[0:1, e:e + 1], min_val=0, max_val=MAXTILES)
                hi = sp.value_load(first[0:1, e + 1:e + 2], min_val=0, max_val=MAXTILES)
                sp.wait_ge(s_tails[e], 16)
                with sp.Fori(lo, hi) as t:
                    sp.wait_ge(s_xt, t + 1)
                    sp.wait_ge(s_id, t + 1)
                    row = nc.s_assert_within(e * REGION + (t - lo) * TILE, 0, E * REGION - TILE)
                    sp.dma_start(xin[:, :], slots[bass.ds(row, TILE), :]).then_inc(s_in, 16)
            total = sp.value_load(first[0:1, E:E + 1], min_val=1, max_val=MAXTILES)
            sp.wait_ge(s_xt, total + 1)
            sp.wait_ge(s_id, total + 1)
            sp.dma_start(xin[:, :], slots[0:TILE, :]).then_inc(s_in, 16)
            added = sp.to_reg(16 * total)
            sp.wait_ge(s_out, 16 * (NPAIR + 1))
            sp.wait_ge(s_add, added)

        @block.tensor
        def _(pe):
            def quad(n):
                return n // (H // QH), n % (H // QH)

            def scores(i, n):
                N = NQ * i + n
                b, s = quad(n)
                c = s * QH // HC
                h = s * QH % HC
                if n == 0:
                    pe.wait_ge(s_qrot, i + 1)
                    pe.wait_ge(s_kblk, 16 * H * (i + 1))
                if N >= 3:
                    pe.wait_ge(s_p, N - 2)
                o = b_s[N % 3][0:S, 0:QH * S]
                pe.matmul(o, ident_bf[0:S, 0:S], mask_bf[0:S].rearrange("p h s -> p (h s)"),
                          start=True, stop=False)
                pe.matmul(o, qrot[:, i % 2, 2 * c + b, :],
                          kblk[:, i % 2, c, h:h + QH, b * S:(b + 1) * S],
                          start=False, stop=True).then_inc(s_s, 1)

            def probs_transpose(N):
                pe.wait_ge(s_p, N + 1)
                if N:
                    pe.wait_ge(s_pTc, N)
                for h in range(QH):
                    m = pe.transpose(b_pt[0:S, h * S:(h + 1) * S], probs[:, N % 3, h, :], ident[0:S, 0:S])
                m.then_inc(s_pT, 1)

            def values(N):
                i, n = divmod(N, NQ)
                b, s = quad(n)
                c = s * QH // HC
                pe.wait_ge(s_pTc, N + 1)
                if n == 0:
                    pe.wait_ge(s_vc, i + 1)
                if s == 0 and 2 * i + b:
                    pe.wait_ge(s_att, 2 * i + b)
                for g in range(QH // 2):
                    j = (s * QH % HC) // 2 + g
                    m = pe.matmul(b_pv[32 * j:32 * j + 32, c * PT:(c + 1) * PT],
                                  v_sb[:, i % 2, b, c * P + 32 * j:c * P + 32 * j + 32],
                                  probsT[:, N % 2, 2 * g:2 * g + 2, :],
                                  start=True, stop=True)
                m.then_inc(s_pv, 1)

            def xn_transpose(i):
                pe.wait_ge(s_xn, i + 1)
                small_free()
                for b in range(2):
                    for c in range(DC):
                        m = pe.transpose(b_small[:, (2 * c + b) * S:(2 * c + b + 1) * S],
                                         xn[:, b, c * P:(c + 1) * P], ident[0:S, 0:S])
                m.then_inc(s_xnT, 1)
                small_use(s_xnTc, i + 1)

            last_small = []

            def small_free():
                if last_small:
                    pe.wait_ge(*last_small[0])

            def small_use(s, v):
                last_small[:] = [(s, v)]

            def project(i, w, rhs, done):
                for c in range(DC):
                    for k in range(DC):
                        m = pe.matmul(b_proj[:, c * PT:(c + 1) * PT], w[:, k, c * P:(c + 1) * P], rhs(k),
                                      start=(k == 0), stop=(k == DC - 1))
                m.then_inc(done, 1)

            def k_project(i):
                if i == 0:
                    pe.wait_ge(s_wk, 16)
                pe.wait_ge(s_ctx[min(i, 1)], 16)
                if i >= 1:
                    pe.wait_ge(s_vc, i)
                project(i, wk, lambda k: ctx_all[:, k, tokens(i)], s_k)

            def q_project(i):
                if i == 0:
                    pe.wait_ge(s_w, 16 * 3)
                pe.wait_ge(s_xnTc, i + 1)
                pe.wait_ge(s_kc, i + 1)
                project(i, wq, lambda k: xnT[:, k, :], s_q)

            def v_project(i):
                pe.wait_ge(s_qc, i + 1)
                for b in range(2):
                    for k in range(DC):
                        t = i * PT + b * S
                        m = pe.matmul(b_proj[0:S, b * D:(b + 1) * D], ctx_all[:, k, t:t + S], wv[:, k, :],
                                      start=(k == 0), stop=(k == DC - 1))
                m.then_inc(s_v, 1)

            def den_transpose(r):
                pe.wait_ge(s_rx, r + 1)
                small_free()
                for c in range(DC):
                    m = pe.transpose(b_small[:, c * S:(c + 1) * S],
                                     rdenx[:, c * HC:(c + 1) * HC, :].rearrange("p h d -> p (h d)"),
                                     ident[0:S, 0:S])
                m.then_inc(s_rT, 1)
                small_use(s_rTc, r + 1)

            def o_project(r):
                i, b = divmod(r, 2)
                pe.wait_ge(s_att, r + 1)
                if b == 0 and i:
                    pe.wait_ge(s_x2, i)
                for k in range(DC):
                    m = pe.matmul(b_o[0:S, b * D:(b + 1) * D], att[:, b, k, :], wo[:, k, :],
                                  start=(k == 0), stop=(k == DC - 1))
                m.then_inc(s_o, 1)

            def x2_transpose(i):
                pe.wait_ge(s_xr, i + 1)
                small_free()
                for b in range(2):
                    for c in range(DC):
                        m = pe.transpose(b_small[:, (2 * b + c) * S:(2 * b + c + 1) * S],
                                         xrow[:, i % 2, b, c * P:(c + 1) * P], ident[0:S, 0:S])
                m.then_inc(s_x2T, 1)
                small_use(s_x2Tc, i + 1)

            def route_logits(i):
                pe.wait_ge(s_x2Tc, i + 1)
                small_free()
                for b in range(2):
                    for c in range(DC):
                        m = pe.matmul(b_small[0:S, b * E:(b + 1) * E], xn2T[:, b, c, :], rw_sb[:, c, :],
                                      start=(c == 0), stop=(c == DC - 1))
                m.then_inc(s_lg, 1)
                small_use(s_lgc, i + 1)

            def ranks(i):
                pe.wait_ge(s_ch, i + 1)
                small_free()
                o = b_small[0:S, 0:2 * E]
                pe.matmul(o, tri_bf[0:S, 0:S], chosen[:, :, :].rearrange("p b e -> p (b e)"),
                          start=True, stop=False)
                pe.matmul(o, ones_bf[0:S, 0:S], before[:, 0:2, :].rearrange("p b e -> p (b e)"),
                          start=False, stop=True).then_inc(s_rk, 1)
                small_use(s_rkc, i + 1)

            pe.wait_ge(s_cst, 16)
            pe.wait_ge(s_setup, 4)
            for i in range(-1, NPAIR + 2):
                cur, nxt, prv, old = 0 <= i < NPAIR, i + 1 < NPAIR, 0 <= i - 1 < NPAIR, 0 <= i - 2
                for n in range(NQ):
                    N = NQ * i + n
                    ready = 0 <= N - 3 < NQ * NPAIR
                    if ready and (N - 3) % 4 == 3:
                        values(N - 3)
                    if cur:
                        scores(i, n)
                    if n == 5 and old:
                        ranks(i - 2)
                    if 0 <= N - 2 < NQ * NPAIR:
                        probs_transpose(N - 2)
                    if n == 0 and prv:
                        o_project(2 * i - 2)
                    if n == 0 and nxt:
                        xn_transpose(i + 1)
                    if n == 1 and nxt:
                        k_project(i + 1)
                    if n == 2 and old:
                        route_logits(i - 2)
                    if n == 3 and nxt:
                        q_project(i + 1)
                    if n == 3 and prv:
                        o_project(2 * i - 1)
                    if n == 5 and nxt:
                        v_project(i + 1)
                    if n == 6 and cur:
                        den_transpose(2 * i)
                    if n == 7 and prv:
                        x2_transpose(i - 1)
                    if ready and (N - 3) % 4 != 3:
                        values(N - 3)
                    if n == 1 and prv:
                        den_transpose(2 * i - 1)

            pe.wait_ge(s_ch, NPAIR)
            small_free()
            pe.matmul(b_small[:, 0:E], ones_bf[0:S, :], before[:, 2, :],
                      start=True, stop=True).then_inc(s_cnt, 1)
            pe.wait_ge(s_wacc, 1)
            pe.matmul(b_o[:, 0:E], cst[0:S, C_ONE:C_ONE + P], wacc[:, :],
                      start=True, stop=True).then_inc(s_wsum, 1)

            def tile_transpose(t):
                pe.wait_ge(s_in, 16 * (t + 1))
                for c in range(DC):
                    m = pe.transpose(b_xt[:, c * TILE:(c + 1) * TILE], xin[:, c * P:(c + 1) * P], ident)
                m.then_inc(s_xt, 1)

            pe.wait_ge(s_first, 1)
            tile_transpose(0)
            with pe.Fori(0, E // 2) as ep:
                for par in range(2):
                    gate, up, down = wpart(par)
                    e = 2 * ep + par
                    lo = pe.value_load(first[0:1, bass.ds(e, 1)], min_val=0, max_val=MAXTILES)
                    hi = pe.value_load(first[0:1, bass.ds(e + 1, 1)], min_val=0, max_val=MAXTILES)
                    loaded = pe.to_reg(16 * (ep + 1))
                    pe.wait_ge(s_first, 1)
                    pe.wait_ge(s_ew[par], loaded)
                    with pe.Fori(lo, hi) as t:
                        pe.wait_ge(s_xtc, t + 1)
                        for half in range(2):
                            for w, banks, done in ((gate, b_gate, s_gate), (up, b_up, s_up)):
                                for f in range(HF):
                                    j = (half * HF + f) * P
                                    for c in range(DC):
                                        m = pe.matmul(banks[half][:, f * TILE:(f + 1) * TILE],
                                                      w[:, c, j:j + P], xT[:, c, :],
                                                      start=(c == 0), stop=(c == DC - 1))
                                m.then_inc(done, 1)
                        for half in range(2):
                            pe.wait_ge(s_h, 2 * t + half + 2)
                            if half == 0:
                                pe.wait_ge(s_y, t + 1)
                            for f in range(half * HF, (half + 1) * HF):
                                m = pe.matmul(b_y[:, 0:D], hT[:, f, :], down[:, f, :],
                                              start=(f == 0), stop=(f == FC - 1))
                            if half == 0:
                                m.then_inc(s_down, 1)
                                tile_transpose(t + 1)
                            else:
                                m.then_inc(s_down, 1)

        @block.scalar
        def _(act_e):
            a = act_e
            a.dma_start(attw[:, 1], wT[:, 1]).then_inc(s_wk, 16)
            a.dma_start(attw[:, 0], wT[:, 0]).then_inc(s_w, 16)
            a.dma_start(attw[:, 2:4], wT[:, 2:4]).then_inc(s_w, 16)
            a.dma_start(attb[:, :, :], bT).then_inc(s_w, 16)
            a.dma_start(biasrow[:, :, :], brow).then_inc(s_x[0], 16)
            a.dma_start(rw_sb[:, :, :], rwT).then_inc(s_x[0], 16)
            a.dma_start(rows_sb[:, :], rownum).then_inc(s_x[0], 16)
            for par in range(2):
                a.dma_start(wbuf[:, par], ffw[par]).then_inc(s_ew[par], 16)

            def evac_proj(i, which, ready, done):
                a.wait_ge(ready, i + 1)
                if i >= 1:
                    a.wait_ge(s_krot if which else s_qrot, i)
                for c in range(DC):
                    m = nc.scalar.activation(proj[:, which, 2 * c:2 * c + 2, :],
                                             b_proj[:, c * PT:(c + 1) * PT].rearrange("p (b s) -> p b s", b=2),
                                             ACT.Identity, bias=attb[:, which, c:c + 1])
                m.then_inc(done, 1)

            def den_copy(r):
                a.wait_ge(s_rT, r + 1)
                if r >= 1:
                    a.wait_ge(s_att, r)
                nc.scalar.copy(rdenT[:, :, :].rearrange("p c s -> p (c s)"),
                               b_small[:, 0:DC * S]).then_inc(s_rTc, 1)

            a.wait_ge(s_w, 16 * 3)
            for i in range(-1, NPAIR + 2):
                cur, nxt, prv = 0 <= i < NPAIR, i + 1 < NPAIR, 0 <= i - 1 < NPAIR
                for n in range(NQ):
                    N = NQ * i + n
                    if n == 2 and prv:
                        den_copy(2 * i - 1)
                    if 0 <= N - 2 < NQ * NPAIR:
                        M = N - 2
                        a.wait_ge(s_pT, M + 1)
                        if M >= 2:
                            a.wait_ge(s_pv, M - 1)
                        nc.scalar.copy(probsT[:, M % 2].rearrange("p h s -> p (h s)"),
                                       b_pt[0:S, 0:QH * S]).then_inc(s_pTc, 1)
                    if n == 6 and cur:
                        den_copy(2 * i)
                    if cur:
                        a.wait_ge(s_max, N + 1)
                        if N >= 3:
                            a.wait_ge(s_pT, N - 2)
                        r = 2 * i + n // 4
                        if n % 4 == 0 and r >= 2:
                            a.wait_ge(s_rx, r - 1)
                        for h in range(QH):
                            k = n % 4 * QH + h
                            m = nc.scalar.activation(probs[:, N % 3, h, :], b_s[N % 3][0:S, h * S:(h + 1) * S],
                                                     ACT.Exp, bias=negmax[:, N % 4, h:h + 1],
                                                     accum_out=psums[:, r % 2, k:k + 1])
                        m.then_inc(s_p, 1)
                    if n == 1 and nxt:
                        evac_proj(i + 1, 1, s_k, s_kc)
                    if n == 0 and nxt:
                        a.wait_ge(s_xnT, i + 2)
                        if i >= 0:
                            a.wait_ge(s_q, i + 1)
                        nc.scalar.copy(xnT[:, :, :].rearrange("p c t -> p (c t)"),
                                       b_small[:, 0:DC * PT]).then_inc(s_xnTc, 1)
                    if n == 3 and nxt:
                        evac_proj(i + 1, 0, s_q, s_qc)
                    if n == 7 and prv:
                        a.wait_ge(s_x2T, i)
                        if i >= 2:
                            a.wait_ge(s_lg, i - 1)
                        nc.scalar.copy(xn2T[:, :, :, :].rearrange("p b c s -> p (b c s)"),
                                       b_small[:, 0:DC * PT]).then_inc(s_x2Tc, 1)

            a.wait_ge(s_dl, 1)
            nc.scalar.activation(etop[:, :, :], delta[:, :, :], ACT.Exp).then_inc(s_et, 1)

            a.wait_ge(s_first, 1)

            def expert_silu(e):
                lo = a.value_load(first[0:1, bass.ds(e, 1)], min_val=0, max_val=MAXTILES)
                hi = a.value_load(first[0:1, bass.ds(e + 1, 1)], min_val=0, max_val=MAXTILES)
                with a.Fori(lo, hi) as t:
                    for half in range(2):
                        a.wait_ge(s_gate, 2 * t + half + 1)
                        a.wait_ge(s_h, 2 * t + half + 1)
                        nc.scalar.activation(act[:, half].rearrange("p f t -> p (f t)"),
                                             b_gate[half][:, :], ACT.Silu).then_inc(s_act, 1)
                return hi

            with a.Fori(0, E // 2 - 1) as ep:
                for par in range(2):
                    e = 2 * ep + par
                    hi = expert_silu(e)
                    a.wait_ge(s_down, 2 * hi + 1)
                    a.dma_start(wbuf[:, par], ffw[bass.ds(e + 2, 1)].rearrange("e p n -> (e p) n")
                                ).then_inc(s_ew[par], 16)
            for e in range(E - 2, E):
                expert_silu(e)

        @block.vector
        def _(v):
            V = nc.vector
            links = [0]

            def link(ins):
                links[0] += 1
                ins.then_inc(dve, 1)
                v.wait_ge(dve, links[0])

            def bc(ap, shape):
                return ap.to_broadcast(shape)

            v.wait_ge(s_cst, 16)
            V.tensor_copy(ident_bf[:, :], cst[:, C_ID:C_ID + P]).then_inc(s_setup, 1)
            V.tensor_copy(tri_bf[:, :], cst[:, C_TRI:C_TRI + P]).then_inc(s_setup, 1)
            V.tensor_copy(ones_bf[:, :], cst[:, C_ONE:C_ONE + P]).then_inc(s_setup, 1)
            V.tensor_copy(mask_bf[:, :, :],
                          bc(cst[:, C_MASK:C_MASK + S].unsqueeze(1), [P, QH, S])).then_inc(s_setup, 1)
            link(V.memset(before[:, :, :], 0.0))

            def norm_stats(src, st, m, done):
                for b in range(2):
                    V.bn_stats(st[:, b, :], src[:, b, :]).then_inc(dve, 1)
                    links[0] += 1
                v.wait_ge(dve, links[0])
                for b in range(2):
                    ins = V.bn_aggr(m[:, b, :], st[:, b, :])
                ins.then_inc(done, 1)

            def xn_stats(i):
                v.wait_ge(s_x[min(i, 1)], 16 if i else 64)
                norm_stats(x_all[:, 2 * i:2 * i + 2, :], stats, mv, s_var)

            def xn_write(i):
                v.wait_ge(s_rstd, i + 1)
                if i:
                    v.wait_ge(s_xnT, i)
                for b in range(2):
                    ins = V.tensor_scalar(xn[:, b, :], x_all[:, 2 * i + b, :], mv[:, b, 0:1], rstd[:, b:b + 1],
                                          ALU.subtract, ALU.mult)
                ins.then_inc(s_xn, 1)

            rope = cst[:, C_ROPE:C_ROPE + 4 * S].rearrange("p (t s) -> p t s", t=4)

            def rotate(i, which, ready, o, done):
                v.wait_ge(ready, i + 1)
                src, sw = proj[:, which], swap[:, which]
                link(V.stream_shuffle(sw, src, [p ^ (DH // 2) for p in range(32)]))
                V.tensor_tensor(src, src, bc(rope[:, 2 * which:2 * which + 1, :], [P, 2 * DC, S]), ALU.mult)
                link(V.tensor_tensor(sw, sw, bc(rope[:, 2 * which + 1:2 * which + 2, :], [P, 2 * DC, S]), ALU.mult))
                V.tensor_tensor(o, src, sw, ALU.add).then_inc(done, 1)

            def k_rotate(i):
                if i:
                    v.wait_ge(s_kblk, 16 * H * i)
                rotate(i, 1, s_kc, krot[:, :, :], s_krot)

            def q_rotate(i):
                if i >= 2:
                    v.wait_ge(s_s, NQ * (i - 1))
                rotate(i, 0, s_qc, qrot[:, i % 2], s_qrot)

            def v_write(i):
                v.wait_ge(s_v, i + 1)
                if i >= 2:
                    v.wait_ge(s_pv, NQ * (i - 1))
                V.tensor_tensor(v_sb[:, i % 2], b_proj[0:S, 0:2 * D].rearrange("p (b d) -> p b d", b=2),
                                bc(biasrow[:, 0:1, :], [S, 2, D]), ALU.add).then_inc(s_vc, 1)

            def den(r):
                v.wait_ge(s_p, 4 * r + 4)
                link(V.reciprocal(rden[:, r % 2, :], psums[:, r % 2, :]))
                if r:
                    v.wait_ge(s_rT, r)
                V.tensor_copy(rdenx[:, :, :], bc(rden[:, r % 2, :].unsqueeze(2), [S, H, DH])).then_inc(s_rx, 1)

            def attend(r):
                b = r % 2
                v.wait_ge(s_pv, 4 * r + 4)
                v.wait_ge(s_rTc, r + 1)
                pv = b_pv[:, 0:DC * PT].rearrange("p (c h s) -> p c h s", c=DC, h=2)
                V.scalar_tensor_tensor(out=ev0[:, :, :], in0=pv[:, :, 0, :], scalar=cst[:, C_PAR:C_PAR + 1],
                                       in1=rdenT[:, :, :], op0=ALU.mult, op1=ALU.mult)
                link(V.scalar_tensor_tensor(out=ev1[:, :, :], in0=pv[:, :, 1, :],
                                            scalar=cst[:, C_PAR + 1:C_PAR + 2],
                                            in1=rdenT[:, :, :], op0=ALU.mult, op1=ALU.mult))
                if r >= 2:
                    v.wait_ge(s_o, r - 1)
                V.tensor_tensor(att[:, b], ev0[:, :, :], ev1[:, :, :], ALU.add).then_inc(s_att, 1)

            def residual(i):
                v.wait_ge(s_o, 2 * i + 2)
                xs = x_all[:, 2 * i:2 * i + 2, :]
                v.wait_ge(s_xob, i + 1)
                ins = V.tensor_tensor(xs, b_o[0:S, 0:2 * D].rearrange("p (b d) -> p b d", b=2), xs, ALU.add)
                ins.then_inc(s_x2, 1)
                v.wait_ge(s_x2, i + 1)
                norm_stats(xs, stats2, mv2, s_var2)

            def rows_write(i):
                v.wait_ge(s_rstd2, i + 1)
                if i >= 2:
                    v.wait_ge(s_scat[i % 2], 16 * TOPK * 2 * (i // 2))
                for b in range(2):
                    V.tensor_copy(xrow[:, i % 2, b, D:RW].bitcast(I32), rows_sb[0:S, 2 * i + b:2 * i + b + 1])
                    ins = V.tensor_scalar(xrow[:, i % 2, b, 0:D], x_all[:, 2 * i + b, :], mv2[:, b, 0:1],
                                          rstd2[:, b:b + 1], ALU.subtract, ALU.mult)
                ins.then_inc(s_xr, 1)

            def choose(i):
                v.wait_ge(s_lg, i + 1)
                V.tensor_copy(logits[:, :, :].rearrange("p b e -> p (b e)"), b_small[0:S, 0:2 * E]).then_inc(s_lgc, 1)
                v.wait_ge(s_lgc, i + 1)
                for b in range(2):
                    V.max(top[:, i, b, :], logits[:, b, :]).then_inc(dve, 1)
                    links[0] += 1
                v.wait_ge(dve, links[0])
                for b in range(2):
                    V.max_index(topi[:, b, :], top[:, i, b, :], logits[:, b, :]).then_inc(dve, 1)
                    links[0] += 1

            def choose_masks(i):
                v.wait_ge(dve, links[0])
                link(V.tensor_copy(choice[:, :, :].rearrange("p k b -> p b k"), topi[:, :, 0:TOPK]))
                m = sel[:, i]
                V.tensor_copy(before[:, 0, :], before[:, 2, :])
                link(V.tensor_tensor(m, bc(cst[0:S, C_EXP:C_EXP + E].unsqueeze(1), [S, 4, E]),
                                     bc(choice[:, :, :].rearrange("p k b -> p (k b)").unsqueeze(2), [S, 4, E]),
                                     ALU.is_equal))

            def choose_counts(i):
                m = sel[:, i]
                link(V.tensor_tensor(chosen[:, :, :], m[:, 0:2, :], m[:, 2:4, :], ALU.add))
                link(V.tensor_tensor(before[:, 1, :], before[:, 0, :], chosen[:, 0, :], ALU.add))
                V.tensor_tensor(before[:, 2, :], before[:, 1, :], chosen[:, 1, :], ALU.add).then_inc(s_ch, 1)

            def places(i):
                v.wait_ge(s_rk, i + 1)
                V.tensor_tensor(place[:, :, :], b_small[0:S, 0:2 * E].rearrange("p (b e) -> p b e", b=2),
                                bc(cst[0:S, C_BASE:C_BASE + E].unsqueeze(1), [S, 2, E]), ALU.add
                                ).then_inc(s_rkc, 1)
                v.wait_ge(s_rkc, i + 1)
                m = sel[:, i]
                for k in range(TOPK):
                    ins = V.tensor_tensor(placed[:, 2 * k:2 * k + 2, :], m[:, 2 * k:2 * k + 2, :], place[:, :, :], ALU.mult)
                link(ins)
                link(V.tensor_reduce(dest[:, :], placed[:, :, :], AX.X, ALU.add))
                if i >= 2:
                    v.wait_ge(s_scat[i % 2], 16 * TOPK * 2 * (i // 2))
                V.tensor_copy(desti[:, i % 2, :], dest[:, :]).then_inc(s_dest, 1)

            for n, free in enumerate((s_xt, s_id, s_y, s_h, s_down, s_idnow)):
                V.memset(credit[:, n:n + 1], 0.0).then_inc(free, 1)
            xn_stats(0)
            for i in range(-1, NPAIR + 2):
                cur, nxt, prv, old = 0 <= i < NPAIR, i + 1 < NPAIR, 0 <= i - 1 < NPAIR, 0 <= i - 2
                for n in range(NQ):
                    N = NQ * i + n
                    if cur:
                        v.wait_ge(s_s, N + 1)
                        if N >= 4:
                            v.wait_ge(s_p, N - 3)
                        V.tensor_reduce(negmax[:, N % 4, :],
                                        b_s[N % 3][0:S, 0:QH * S].rearrange("p (h s) -> p h s", h=QH),
                                        AX.X, ALU.max, negate=True).then_inc(s_max, 1)
                    if n == 0 and nxt:
                        xn_write(i + 1)
                    if n == 1 and prv:
                        den(2 * i - 1)
                    if n == 2 and prv:
                        attend(2 * i - 1)
                    if n == 2 and nxt:
                        k_rotate(i + 1)
                    if n == 3 and old:
                        choose(i - 2)
                        choose_masks(i - 2)
                    if n == 4 and old:
                        choose_counts(i - 2)
                    if n == 4 and nxt:
                        q_rotate(i + 1)
                    if n == 5 and old:
                        places(i - 2)
                    if n == 5 and cur:
                        den(2 * i)
                    if n == 5 and prv:
                        residual(i - 1)
                    if n == 6 and cur:
                        attend(2 * i)
                    if n == 6 and prv:
                        rows_write(i - 1)
                    if n == 7 and nxt:
                        v_write(i + 1)
                    if n == 7 and i + 2 < NPAIR:
                        xn_stats(i + 2)

            V.tensor_tensor(delta[:, :, :].rearrange("p k t -> p t k"),
                            top[:, :, :, 0:TOPK].rearrange("p i b k -> p (i b) k"),
                            bc(top[:, :, :, 0:1].rearrange("p i b k -> p (i b) k"), [S, B, TOPK]),
                            ALU.subtract).then_inc(s_dl, 1)
            v.wait_ge(s_cnt, 1)
            link(V.tensor_copy(cnt[:, :], b_small[:, 0:E]))
            V.tensor_tensor(taili[:, :], cnt[:, :], cst[:, C_TAIL:C_TAIL + E], ALU.add).then_inc(s_tail, 1)
            link(V.tensor_tensor(over[:, :, :], bc(cnt[0:1, :].unsqueeze(2), [1, E, MAXT - 1]),
                                 cst[0:1, C_THR:C_LT].rearrange("p (e j) -> p e j", e=E), ALU.is_gt))
            link(V.tensor_reduce(ntile[:, :], over[:, :, :], AX.X, ALU.add))
            link(V.tensor_scalar(ntile1[:, :], ntile[:, :], 1.0, None, ALU.add))
            link(V.tensor_tensor(upto[:, :, :], bc(ntile1[:, :].unsqueeze(1), [1, E + 1, E]),
                                 cst[0:1, C_LT:C_ALL].rearrange("p (j e) -> p j e", e=E), ALU.mult))
            link(V.tensor_reduce(first_f[:, :], upto[:, :, :], AX.X, ALU.add))
            V.tensor_copy(first[:, :], first_f[:, :]).then_inc(s_first, 1)
            link(V.tensor_scalar(cnt1[:, :], cnt[:, :], 1.0, None, ALU.max))
            link(V.reciprocal(crec[:, :], cnt1[:, :]))
            v.wait_ge(s_et, 1)
            link(V.tensor_tensor(esum[:, :], etop[:, 0, :], etop[:, 1, :], ALU.add))
            link(V.reciprocal(erec[:, :], esum[:, :]))
            link(V.tensor_tensor(wtop[:, :, :], etop[:, :, :], bc(erec[:, :].unsqueeze(1), [S, TOPK, B]), ALU.mult))
            for k in range(TOPK):
                ins = V.tensor_tensor(wsel[:, :, 2 * k:2 * k + 2, :], sel[:, :, 2 * k:2 * k + 2, :],
                                      bc(wtop[:, k, :].rearrange("p (i b) -> p i b", b=2).unsqueeze(3),
                                         [S, NPAIR, 2, E]), ALU.mult)
            link(ins)
            V.tensor_reduce(wacc[:, :], wsel[:, :, :, :].rearrange("p i k e -> p e (i k)"), AX.X,
                            ALU.add).then_inc(s_wacc, 1)
            v.wait_ge(s_wsum, 1)
            link(V.tensor_tensor(meanw[:, :], b_o[:, 0:E], crec[:, :], ALU.mult))

            v.wait_ge(s_first, 1)

            def copy_xt(t):
                v.wait_ge(s_xt, t + 2)
                V.tensor_copy(xT[:, :, :].rearrange("p c t -> p (c t)"), b_xt[:, 0:DC * TILE]).then_inc(s_xtc, 1)
                v.wait_ge(s_in, 16 * (t + 1))
                v.wait_ge(s_idnow, t + 1)
                V.tensor_copy(idnext[:, :], xin[:, D:RW].bitcast(I32)).then_inc(s_id, 1)

            copy_xt(0)
            with v.Fori(0, E) as e:
                lo = v.value_load(first[0:1, bass.ds(e, 1)], min_val=0, max_val=MAXTILES)
                hi = v.value_load(first[0:1, bass.ds(e + 1, 1)], min_val=0, max_val=MAXTILES)
                with v.Fori(lo, hi) as t:
                    for half in range(2):
                        v.wait_ge(s_up, 2 * t + half + 1)
                        v.wait_ge(s_act, 2 * t + half + 1)
                        v.wait_ge(s_down, 2 * t + 1)
                        V.tensor_tensor(hT[:, half * HF:(half + 1) * HF, :].rearrange("p f t -> p (f t)"),
                                        b_up[half][:, :], act[:, half].rearrange("p f t -> p (f t)"),
                                        ALU.mult).then_inc(s_h, 1)
                    copy_xt(t + 1)
                    v.wait_ge(s_down, 2 * t + 3)
                    v.wait_ge(s_idnow, t + 2)
                    V.tensor_scalar(y_sb[:, :], b_y[:, 0:D], meanw[:, bass.ds(e, 1)], None,
                                    ALU.mult).then_inc(s_y, 1)

        @block.gpsimd
        def _(g):
            G = nc.gpsimd
            G.memset(tailrow[:, :], 0.0).then_inc(s_zero, 1)
            G.memset(eps_exp[:, :], -0.5).then_inc(s_zero, 1)
            G.memset(kblk[:, :, :, :, :].rearrange("p a c h t -> p (a c h t)"), 0.0).then_inc(s_zero, 1)
            ps = [0]

            def inverse_deviation(i, var, m, v_e, o, done, used):
                g.wait_ge(var, i + 1)
                if i:
                    g.wait_ge(used, i)
                G.tensor_scalar(v_e[:, :], m[:, :, 1], EPS, None, ALU.add).then_inc(pool_self, 1)
                ps[0] += 1
                g.wait_ge(pool_self, ps[0])
                G.tensor_tensor(o[:, :], v_e[:, :], eps_exp[0:S, :], ALU.pow).then_inc(done, 1)

            def scatter(i):
                g.wait_ge(s_dest, i + 1)
                for k in range(TOPK):
                    for b in range(2):
                        c = 2 * k + b
                        G.indirect_dma_start(slots, bass.IndirectOffsetOnAxis(desti[:, i % 2, c:c + 1], 0),
                                             xrow[:, i % 2, b, :], None).then_inc(s_scat[i % 2], 16)

            g.wait_ge(s_zero, 3)
            for i in range(-1, NPAIR + 2):
                if i + 1 < NPAIR:
                    if i == -1:
                        inverse_deviation(0, s_var, mv, ve, rstd, s_rstd, s_xn)
                    g.wait_ge(s_xn, i + 2)
                    xs = x_all[:, 2 * i + 2:2 * i + 4, :]
                    G.tensor_tensor(xs, xs, biasrow[:, 1:2, :].to_broadcast([S, 2, D]), ALU.add).then_inc(s_xob, 1)
                if 0 <= i - 1 < NPAIR:
                    inverse_deviation(i - 1, s_var2, mv2, ve2, rstd2, s_rstd2, s_xr)
                if 0 <= i - 2 < NPAIR:
                    scatter(i - 2)
                if i + 2 < NPAIR:
                    inverse_deviation(i + 2, s_var, mv, ve, rstd, s_rstd, s_xn)

            g.wait_ge(s_out, 16)
            G.tensor_copy(tailrow[:, D:RW].bitcast(I32), rows_sb[:, B:B + 1]).then_inc(pool_self, 1)
            ps[0] += 1
            g.wait_ge(pool_self, ps[0])
            g.wait_ge(s_tail, 1)
            for e in range(E):
                G.indirect_dma_start(slots, bass.IndirectOffsetOnAxis(taili[:, e:e + 1], 0),
                                     tailrow[:, :], None).then_inc(s_tails[e], 16)

            g.wait_ge(s_first, 1)
            total = g.value_load(first[0:1, E:E + 1], min_val=1, max_val=MAXTILES)
            g.wait_ge(s_out, 16 * (NPAIR + 1))
            with g.Fori(0, total) as t:
                taken, added = g.to_reg(t + 2), g.to_reg(16 * (t + 1))
                g.wait_ge(s_first, 1)
                g.wait_ge(s_id, taken)
                G.tensor_copy(idnow[:, :], idnext[:, :]).then_inc(s_idnow, 1)
                g.wait_ge(s_first, 1)
                g.wait_ge(s_y, taken)
                g.wait_ge(s_idnow, taken)
                G.indirect_dma_start(out, bass.IndirectOffsetOnAxis(idnow[:, 0:1], 0), y_sb[:, :], None,
                                     bounds_check=TOK + P - 1, oob_is_err=True,
                                     compute_op=ALU.add).then_inc(s_add, 16)
                g.wait_ge(s_first, 1)
                g.wait_ge(s_add, added)


def kernel(**inputs):
    import concourse.bacc as _bacc
    from concourse.bass_utils import run_bass_kernel_spmd as _run

    def arr(n):
        return np.asarray(inputs[n])

    def chunks(w):
        t = np.swapaxes(w, -1, -2)
        t = t.reshape(t.shape[:-2] + (t.shape[-2] // P, P, t.shape[-1]))
        return np.ascontiguousarray(np.swapaxes(t, -3, -2))

    x = np.ascontiguousarray(arr("x"))
    ctxT = np.ascontiguousarray(arr("ctx_1024")[:, :S].reshape(TOK, DC, P).transpose(2, 1, 0))
    wT = np.stack([chunks(arr(f"L0_xattn_{n}_w")) for n in "qkvo"], 1)
    bT = np.stack([arr(f"L0_xattn_{n}_b").reshape(DC, P).T for n in "qk"], 1)
    brow = np.ascontiguousarray(np.broadcast_to(np.stack([arr(f"L0_xattn_{n}_b") for n in "vo"]), (S, 2, D)))
    rwT = chunks(arr("L0_ffn_router_w"))
    ffw = np.concatenate([chunks(arr(f"L0_ffn_{n}_w")).reshape(E, P, -1) for n in ("gate", "up", "down")], -1)
    consts, rownum = shape_constants()
    host = {"x": x, "ctxT": ctxT, "wT": wT, "bT": np.ascontiguousarray(bT), "brow": brow, "rwT": rwT,
            "ffw": ffw, "consts": consts, "rownum": rownum}

    nc = _bacc.Bacc("TRN2", target_bir_lowering=False, num_devices=1)
    args = [nc.dram_tensor(f"in_{k}", a.shape, mybir.dt.from_np(a.dtype), kind="ExternalInput").ap()
            for k, a in host.items()]
    out = nc.dram_tensor("out_0", (TOK + P, D), F32, kind="ExternalOutput").ap()
    build(nc, *args, out)
    r = _run(nc, [{f"in_{k}": a for k, a in host.items()}], core_ids=[0])
    return r.results[0]["out_0"][:TOK].reshape(B, S, D)
```

```python
from contextlib import ExitStack

import numpy as np

import concourse.bass as bass
from concourse import mybir

F32 = mybir.dt.float32
F32R = mybir.dt.float32r
BF16 = mybir.dt.bfloat16
I32 = mybir.dt.int32
U32 = mybir.dt.uint32
ALU = mybir.AluOpType
ACT = mybir.ActivationFunctionType
AX = mybir.AxisListType

B, S, D = 16, 100, 256
H, DH, WINDOW = 16, 16, 64
E, FF, TOPK = 8, 1024, 2
EPS = 1e-5
TOK = B * S
P = 128
DC = D // P
HC = H // DC
FC = FF // P
NPAIR = B // 2
PT = 2 * S
QH = 4
NQ = 2 * H // QH
TILE = 128
MAXT = -(-TOK // TILE)
REGION = MAXT * TILE + TILE
RW = D + 1
MAXTILES = TOPK * TOK // TILE + E
NEG = -1e30
HF = FC // 2
HALF = FF // 2
THIRDS = 3
WT = DC * FF
WC = 512
CH = WT // WC
WCH = THIRDS * CH
WE = THIRDS * WT
FIELD = 6
assert MAXTILES < 1 << FIELD

C_ID, C_TRI, C_ONE, C_MASK = 0, 128, 256, 384
C_ROPE = C_MASK + S
C_PAR = C_ROPE + 4 * S
C_EXP = C_PAR + 2
C_BASE = C_EXP + E
C_TAIL = C_BASE + E
C_THR = C_TAIL + E
C_LT = C_THR + E * (MAXT - 1)
C_ALL = C_LT + (E + 1) * E


def shape_constants():
    c = np.zeros((P, C_ALL), np.float32)
    p = np.arange(P)
    c[:, C_ID:C_ID + P] = np.eye(P)
    c[:, C_TRI:C_TRI + P] = p[:, None] < p[None, :]
    c[:, C_ONE:C_ONE + P] = 1
    k = np.arange(S)
    seen = (k[None, :] <= p[:, None]) & (k[None, :] >= p[:, None] - WINDOW)
    c[:, C_MASK:C_MASK + S] = np.where(seen, 0, NEG)
    half = DH // 2
    freqs = np.float32(1) / np.float32(10000) ** (np.arange(half, dtype=np.float32) / np.float32(half))
    ang = (np.arange(S, dtype=np.float32)[:, None] * freqs[None, :]).astype(np.float32)
    j = p % half
    cos, sin = np.cos(ang).T[j], np.sin(ang).T[j] * np.where(p % DH < half, -1, 1)[:, None]
    for n, (t, scale) in enumerate(((cos, DH ** -0.5), (sin, DH ** -0.5), (cos, 1), (sin, 1))):
        c[:, C_ROPE + n * S:C_ROPE + (n + 1) * S] = t * scale
    c[:, C_PAR] = p // DH % 2 == 0
    c[:, C_PAR + 1] = p // DH % 2 == 1
    c[:, C_EXP:C_EXP + E] = np.arange(E)
    c[:, C_BASE:C_BASE + E] = np.arange(E) * REGION
    c[:, C_TAIL:C_TAIL + E] = np.arange(E) * REGION + p[:, None]
    c[:, C_THR:C_LT] = np.tile(TILE * np.arange(1, MAXT), E)
    c[:, C_LT:C_ALL] = (np.arange(E)[None, :] < np.arange(E + 1)[:, None]).ravel()
    rows = np.zeros((P, B + 1), np.int32)
    rows[:, :B] = np.arange(B)[None, :] * S + p[:, None]
    rows[:, B] = TOK + p
    return c, rows


def build(nc, x, ctxT, wT, bT, brow, rwT, ffw, consts, rownum, out):
    ctx = ExitStack()
    with ctx:
        def sb(name, shape, dt=F32):
            return ctx.enter_context(nc.sbuf_tensor(name, shape, dt))

        def bank(name):
            return ctx.enter_context(nc.psum_tensor(name, [P, 512], F32))

        def sem(name):
            return ctx.enter_context(nc.semaphore(name))

        att_ctx = ctx.enter_context(ExitStack())

        def att_sb(name, shape, dt=F32):
            return att_ctx.enter_context(nc.sbuf_tensor(name, shape, dt))

        slots = nc.dram_tensor("slots", (E * REGION, RW), F32, kind="Internal").ap()

        cst = sb("cst", [P, C_ALL])
        rows_sb = sb("rows_sb", [P, B + 1], I32)
        ident = cst[:, C_ID:C_ID + P]
        ident_bf = sb("ident_bf", [P, P], BF16)
        tri_bf = sb("tri_bf", [P, P], BF16)
        ones_bf = sb("ones_bf", [P, P], BF16)
        mask_bf = sb("mask_bf", [P, QH, S], BF16)
        attb = sb("attb", [P, 2, DC])
        biasrow = sb("biasrow", [S, 2, D])
        rw_sb = sb("rw_sb", [P, DC, E])
        eps_exp = sb("eps_exp", [P, 2])
        x_all = sb("x_all", [S, B, D])
        stats = sb("stats", [S, 2, 6])
        mv = sb("mv", [S, 2, 2])
        ve = sb("ve", [S, 2])
        rstd = sb("rstd", [S, 2])
        negmax = sb("negmax", [S, 4, QH])
        psums = sb("psums", [S, 2, H])
        rden = sb("rden", [S, 2, H])
        stats2 = sb("stats2", [S, 2, 6])
        mv2 = sb("mv2", [S, 2, 2])
        ve2 = sb("ve2", [S, 2])
        rstd2 = sb("rstd2", [S, 2])
        xrow = sb("xrow", [S, 2, 2, RW])
        logits = sb("logits", [S, 2, E])
        top = sb("top", [S, NPAIR, 2, E])
        topi = sb("topi", [S, 2, E], U32)
        choice = sb("choice", [S, TOPK, 2])
        sel = sb("sel", [S, NPAIR, TOPK * 2, E])
        delta = sb("delta", [S, TOPK, B])
        etop = sb("etop", [S, TOPK, B])
        esum = sb("esum", [S, B])
        erec = sb("erec", [S, B])
        wtop = sb("wtop", [S, TOPK, B])
        wsel = sb("wsel", [S, NPAIR, TOPK * 2, E])
        chosen = sb("chosen", [S, 2, E], BF16)
        before = sb("before", [S, 3, E], BF16)
        place = sb("place", [S, 2, E])
        placed = sb("placed", [S, TOPK * 2, E])
        dest = sb("dest", [S, TOPK * 2])
        desti = sb("desti", [S, 2, TOPK * 2], U32)
        wacc = sb("wacc", [S, E])
        credit = sb("credit", [1, 8])
        cnt = sb("cnt", [P, E])
        cnt1 = sb("cnt1", [P, E])
        crec = sb("crec", [P, E])
        meanw = sb("meanw", [P, E])
        taili = sb("taili", [P, E], U32)
        tailrow = sb("tailrow", [P, RW])
        over = sb("over", [1, E, MAXT - 1])
        ntile = sb("ntile", [1, E])
        ntile1 = sb("ntile1", [1, E])
        upto = sb("upto", [1, E + 1, E])
        first_f = sb("first_f", [1, E + 1])
        first = sb("first", [1, E + 1], I32)
        nsplit = sb("nsplit", [1, E])
        mid = sb("mid", [1, E])
        more = sb("more", [1, E])
        plan_a = sb("plan_a", [1, E])
        plan_b = sb("plan_b", [1, E])
        plan = sb("plan", [1, E], I32)
        w_raw0 = sb("w_raw0", [P, WE])
        w_hi0 = sb("w_hi0", [P, WE], F32R)
        w_lo0 = sb("w_lo0", [P, WE], F32R)
        attw = att_sb("attw", [P, 4, DC, D])
        ctx_all = att_sb("ctx_all", [P, DC, TOK])
        xn = att_sb("xn", [S, 2, D])
        xnT = att_sb("xnT", [P, DC, PT])
        proj = att_sb("proj", [P, 2, DC * 2, S])
        swap = att_sb("swap", [P, 2, DC * 2, S])
        krot = att_sb("krot", [P, DC * 2, S])
        qrot = att_sb("qrot", [P, 2, DC * 2, S])
        kblk = att_sb("kblk", [P, 2, DC, HC, PT])
        v_sb = att_sb("v_sb", [S, 2, 2, D])
        probs = att_sb("probs", [S, 3, QH, S])
        rdenx = att_sb("rdenx", [S, H, DH])
        probsT = att_sb("probsT", [S, 3, QH, S])
        rdenT = att_sb("rdenT", [P, DC, S])
        ev0 = att_sb("ev0", [P, DC, S])
        ev1 = att_sb("ev1", [P, DC, S])
        att = att_sb("att", [P, 2, DC, S])
        xn2T = att_sb("xn2T", [P, 2, DC, S])
        att_ctx.close()
        w_raw = [w_raw0, sb("w_raw1", [P, WE])]
        w_hi = [w_hi0, sb("w_hi1", [P, WE], F32R)]
        w_lo = [w_lo0, sb("w_lo1", [P, WE], F32R)]
        xin = sb("xin", [TILE, RW])
        idnext = sb("idnext", [TILE, 2], I32)
        idnow = sb("idnow", [TILE, 1], I32)
        x_hi = sb("x_hi", [P, DC, TILE], F32R)
        x_lo = sb("x_lo", [P, DC, TILE], F32R)
        act = sb("act", [TILE, 2, HALF])
        h_sb = sb("h_sb", [TILE, 2, HALF])
        h_hi = sb("h_hi", [P, FC, TILE], F32R)
        h_lo = sb("h_lo", [P, FC, TILE], F32R)
        mean1 = sb("mean1", [P, 1])
        y_raw = sb("y_raw", [TILE, D])
        y_sb = sb("y_sb", [TILE, D])

        b_small = bank("b_small")
        b_proj = bank("b_proj")
        b_o = bank("b_o")
        b_s = [bank(f"b_s{n}") for n in range(3)]
        b_pt = bank("b_pt")
        b_pv = bank("b_pv")
        b_gate = [b_s[0], b_s[1]]
        b_up = [b_s[2], b_pt]
        b_ht = [b_small, b_o]
        b_y = b_pv
        b_xt = b_proj

        wq, wk, wv, wo = (attw[:, n] for n in range(4))

        def tiles_of(engine, e):
            mask = (1 << FIELD) - 1
            word = engine.value_load(plan[0:1, bass.ds(e, 1)], min_val=0, max_val=(1 << 3 * FIELD + 1) - 1)
            lo, hi, m = (engine.snap((word >> n * FIELD) & mask if n else word & mask) for n in range(3))
            return lo, hi, engine.snap((hi - 1) & mask), m, engine.snap(word >> 3 * FIELD)

        def wpart(w):
            return (w[:, 0:WT].rearrange("p (c f) -> p c f", c=DC),
                    w[:, WT:2 * WT].rearrange("p (c f) -> p c f", c=DC),
                    w[:, 2 * WT:3 * WT].rearrange("p (f d) -> p f d", d=D))

        s_cst = sem("s_cst")
        s_wk = sem("s_wk")
        s_w = sem("s_w")
        s_x = [sem(f"s_xin{i}") for i in range(3)]
        s_ctx = [sem(f"s_ctx{i}") for i in range(3)]
        s_setup = sem("s_setup")
        s_zero = sem("s_zero")
        dve = sem("dve")
        pool_self = sem("pool_self")
        s_var = sem("s_var")
        s_rstd = sem("s_rstd")
        s_xn = sem("s_xn")
        s_xnT = sem("s_xnT")
        s_xnTc = sem("s_xnTc")
        s_k = sem("s_k")
        s_kc = sem("s_kc")
        s_q = sem("s_q")
        s_qc = sem("s_qc")
        s_v = sem("s_v")
        s_vc = sem("s_vc")
        s_krot = sem("s_krot")
        s_kblk = [sem(f"s_kblk{c}") for c in range(DC)]
        s_qrot = sem("s_qrot")
        s_s = sem("s_s")
        s_max = sem("s_max")
        s_p = sem("s_p")
        s_pT = sem("s_pT")
        s_pTc = sem("s_pTc")
        s_pv = sem("s_pv")
        s_rx = sem("s_rx")
        s_rT = sem("s_rT")
        s_rTc = sem("s_rTc")
        s_att = sem("s_att")
        s_o = sem("s_o")
        s_xob = sem("s_xob")
        s_x2 = sem("s_x2")
        s_out = sem("s_out")
        s_pad = sem("s_pad")
        s_var2 = sem("s_var2")
        s_rstd2 = sem("s_rstd2")
        s_xr = sem("s_xr")
        s_x2T = sem("s_x2T")
        s_x2Tc = sem("s_x2Tc")
        s_lg = sem("s_lg")
        s_lgc = sem("s_lgc")
        s_dl = sem("s_dl")
        s_et = sem("s_et")
        s_ch = sem("s_ch")
        s_rk = sem("s_rk")
        s_rkc = sem("s_rkc")
        s_dest = sem("s_dest")
        s_scat = [sem(f"s_scat{i}") for i in range(2)]
        s_wacc = sem("s_wacc")
        s_cnt = sem("s_cnt")
        s_wsum = sem("s_wsum")
        s_mean = sem("s_mean")
        s_scaled = sem("s_scaled")
        s_tail = sem("s_tail")
        s_tails = [sem(f"s_tails{e}") for e in range(E)]
        s_first = sem("s_first")
        s_raw = [sem(f"s_raw{i}") for i in range(2)]
        s_whi = sem("s_whi")
        s_wlo = sem("s_wlo")
        s_in = sem("s_in")
        s_xt = sem("s_xt")
        s_xhi = sem("s_xhi")
        s_xlo = sem("s_xlo")
        s_id = sem("s_id")
        s_gate = sem("s_gate")
        s_up = sem("s_up")
        s_act = sem("s_act")
        s_h = sem("s_h")
        s_ht = sem("s_ht")
        s_hhi = sem("s_hhi")
        s_hlo = sem("s_hlo")
        s_down = sem("s_down")
        s_y = sem("s_y")
        s_add = sem("s_add")
        s_idnow = sem("s_idnow")

        block = ctx.enter_context(nc.Block())
        pairs = range(NPAIR)

        def tokens(i):
            return slice(i * PT, (i + 1) * PT)

        @block.sync
        def _(sp):
            def load_rows(n, lo, hi):
                sp.dma_start(ctx_all[:, :, lo * PT:hi * PT], ctxT[:, :, lo * PT:hi * PT]).then_inc(s_ctx[n], 16)
                sp.dma_start(x_all[:, 2 * lo:2 * hi, :], x[2 * lo:2 * hi].rearrange("b s d -> s b d")
                             ).then_inc(s_x[n], 16)

            load_rows(0, 0, 1)
            sp.dma_start(cst[:, :], consts).then_inc(s_cst, 16)
            load_rows(1, 1, 2)
            sp.wait_ge(s_zero, 2)
            sp.dma_start(out[TOK:TOK + P, :], tailrow[:, 0:D]).then_inc(s_pad, 16)

            def key_blocks(i):
                sp.wait_ge(s_krot, i + 1)
                if i >= 2:
                    sp.wait_ge(s_s, NQ * (i - 1))
                for c in range(DC):
                    for h in range(HC):
                        r = slice(h * DH, (h + 1) * DH)
                        sp.dma_start(kblk[r, i % 2, c, h, :],
                                     krot[r, 2 * c:2 * c + 2, :].rearrange("p b s -> p (b s)")
                                     ).then_inc(s_kblk[c], 16)

            def store_x2(i):
                sp.wait_ge(s_x2, i + 1)
                sp.dma_start(out[tokens(i), :].rearrange("(b s) d -> s b d", b=2),
                             x_all[:, 2 * i:2 * i + 2, :]).then_inc(s_out, 16)

            sp.wait_ge(s_zero, 3)
            key_blocks(0)
            load_rows(2, 2, NPAIR)
            for i in pairs:
                if i + 1 < NPAIR:
                    key_blocks(i + 1)
                if i >= 1:
                    store_x2(i - 1)
            sp.wait_ge(s_wlo, WCH)
            sp.dma_start(w_raw[0][:, :], ffw[1]).then_inc(s_raw[0], 16)
            store_x2(NPAIR - 1)

            sp.wait_ge(s_first, 1)
            for q in s_scat:
                sp.wait_ge(q, 16 * TOPK * 2 * (NPAIR // 2))
            for e in range(E):
                lo = sp.value_load(first[0:1, e:e + 1], min_val=0, max_val=MAXTILES)
                hi = sp.value_load(first[0:1, e + 1:e + 2], min_val=0, max_val=MAXTILES)
                sp.wait_ge(s_tails[e], 16)
                with sp.Fori(lo, hi) as t:
                    sp.wait_ge(s_xt, t + 1)
                    sp.wait_ge(s_id, t + 1)
                    row = nc.s_assert_within(e * REGION + (t - lo) * TILE, 0, E * REGION - TILE)
                    sp.dma_start(xin[:, :], slots[bass.ds(row, TILE), :]).then_inc(s_in, 16)
            total = sp.value_load(first[0:1, E:E + 1], min_val=1, max_val=MAXTILES)
            added = sp.to_reg(16 * total)
            sp.wait_ge(s_pad, 16)
            sp.wait_ge(s_out, 16 * NPAIR)
            sp.wait_ge(s_add, added)

        @block.tensor
        def _(pe):
            def quad(n):
                return n // (H // QH), n % (H // QH)

            def scores(i, n):
                N = NQ * i + n
                b, s = quad(n)
                c = s * QH // HC
                h = s * QH % HC
                if n == 0:
                    pe.wait_ge(s_qrot, i + 1)
                if n in (0, HC // QH):
                    pe.wait_ge(s_kblk[c], 16 * HC * (i + 1))
                if N >= 3:
                    pe.wait_ge(s_p, N - 2)
                o = b_s[N % 3][0:S, 0:QH * S]
                pe.matmul(o, ident_bf[0:S, 0:S], mask_bf[0:S].rearrange("p h s -> p (h s)"),
                          start=True, stop=False)
                pe.matmul(o, qrot[:, i % 2, 2 * c + b, :],
                          kblk[:, i % 2, c, h:h + QH, b * S:(b + 1) * S],
                          start=False, stop=True).then_inc(s_s, 1)

            def probs_transpose(N):
                pe.wait_ge(s_p, N + 1)
                if N:
                    pe.wait_ge(s_pTc, N)
                for h in range(QH):
                    m = pe.transpose(b_pt[0:S, h * S:(h + 1) * S], probs[:, N % 3, h, :], ident[0:S, 0:S])
                m.then_inc(s_pT, 1)

            def values(N):
                i, n = divmod(N, NQ)
                b, s = quad(n)
                c = s * QH // HC
                pe.wait_ge(s_pTc, N + 1)
                if n == 0:
                    pe.wait_ge(s_vc, i + 1)
                if s == 0 and 2 * i + b:
                    pe.wait_ge(s_att, 2 * i + b)
                for g in range(QH // 2):
                    j = (s * QH % HC) // 2 + g
                    m = pe.matmul(b_pv[32 * j:32 * j + 32, c * PT:(c + 1) * PT],
                                  v_sb[:, i % 2, b, c * P + 32 * j:c * P + 32 * j + 32],
                                  probsT[:, N % 3, 2 * g:2 * g + 2, :],
                                  start=True, stop=True)
                m.then_inc(s_pv, 1)

            def xn_transpose(i):
                if i == 0:
                    pe.wait_ge(s_cst, 16)
                    pe.wait_ge(s_setup, 4)
                pe.wait_ge(s_xn, i + 1)
                small_free()
                for b in range(2):
                    for c in range(DC):
                        m = pe.transpose(b_small[:, (2 * c + b) * S:(2 * c + b + 1) * S],
                                         xn[:, b, c * P:(c + 1) * P], ident[0:S, 0:S])
                m.then_inc(s_xnT, 1)
                small_use(s_xnTc, i + 1)

            last_small = []

            def small_free():
                if last_small:
                    pe.wait_ge(*last_small[0])

            def small_use(s, v):
                last_small[:] = [(s, v)]

            def project(i, w, rhs, done):
                for c in range(DC):
                    for k in range(DC):
                        m = pe.matmul(b_proj[:, c * PT:(c + 1) * PT], w[:, k, c * P:(c + 1) * P], rhs(k),
                                      start=(k == 0), stop=(k == DC - 1))
                m.then_inc(done, 1)

            def k_project(i):
                if i == 0:
                    pe.wait_ge(s_wk, 32)
                pe.wait_ge(s_ctx[min(i, 2)], 16)
                if i >= 1:
                    pe.wait_ge(s_vc, i)
                project(i, wk, lambda k: ctx_all[:, k, tokens(i)], s_k)

            def q_project(i):
                if i == 0:
                    pe.wait_ge(s_w, 16 * 5)
                pe.wait_ge(s_xnTc, i + 1)
                pe.wait_ge(s_kc, i + 1)
                project(i, wq, lambda k: xnT[:, k, :], s_q)

            def v_project(i):
                pe.wait_ge(s_qc, i + 1)
                for b in range(2):
                    for k in range(DC):
                        t = i * PT + b * S
                        m = pe.matmul(b_proj[0:S, b * D:(b + 1) * D], ctx_all[:, k, t:t + S], wv[:, k, :],
                                      start=(k == 0), stop=(k == DC - 1))
                m.then_inc(s_v, 1)

            def den_transpose(r):
                pe.wait_ge(s_rx, r + 1)
                small_free()
                for c in range(DC):
                    m = pe.transpose(b_small[:, c * S:(c + 1) * S],
                                     rdenx[:, c * HC:(c + 1) * HC, :].rearrange("p h d -> p (h d)"),
                                     ident[0:S, 0:S])
                m.then_inc(s_rT, 1)
                small_use(s_rTc, r + 1)

            def o_project(r):
                i, b = divmod(r, 2)
                pe.wait_ge(s_att, r + 1)
                if b == 0 and i:
                    pe.wait_ge(s_x2, i)
                for k in range(DC):
                    m = pe.matmul(b_o[0:S, b * D:(b + 1) * D], att[:, b, k, :], wo[:, k, :],
                                  start=(k == 0), stop=(k == DC - 1))
                m.then_inc(s_o, 1)

            def x2_transpose(i):
                pe.wait_ge(s_xr, i + 1)
                small_free()
                for b in range(2):
                    for c in range(DC):
                        m = pe.transpose(b_small[:, (2 * b + c) * S:(2 * b + c + 1) * S],
                                         xrow[:, i % 2, b, c * P:(c + 1) * P], ident[0:S, 0:S])
                m.then_inc(s_x2T, 1)
                small_use(s_x2Tc, i + 1)

            def route_logits(i):
                pe.wait_ge(s_x2Tc, i + 1)
                small_free()
                for b in range(2):
                    for c in range(DC):
                        m = pe.matmul(b_small[0:S, b * E:(b + 1) * E], xn2T[:, b, c, :], rw_sb[:, c, :],
                                      start=(c == 0), stop=(c == DC - 1))
                m.then_inc(s_lg, 1)
                small_use(s_lgc, i + 1)

            def ranks(i):
                pe.wait_ge(s_ch, i + 1)
                small_free()
                o = b_small[0:S, 0:2 * E]
                pe.matmul(o, tri_bf[0:S, 0:S], chosen[:, :, :].rearrange("p b e -> p (b e)"),
                          start=True, stop=False)
                pe.matmul(o, ones_bf[0:S, 0:S], before[:, 0:2, :].rearrange("p b e -> p (b e)"),
                          start=False, stop=True).then_inc(s_rk, 1)
                small_use(s_rkc, i + 1)

            for i in range(-1, NPAIR + 2):
                cur, nxt, prv, old = 0 <= i < NPAIR, i + 1 < NPAIR, 0 <= i - 1 < NPAIR, 0 <= i - 2
                for n in range(NQ):
                    N = NQ * i + n
                    for m in ((N - 4,) if n % 4 == 0 else (N - 3,) if n % 4 == 2 else ()):
                        if 0 <= m < NQ * NPAIR:
                            values(m)
                    if cur:
                        scores(i, n)
                    if n == 5 and 0 <= i - 2 < NPAIR:
                        ranks(i - 2)
                    if n == 2 and prv:
                        den_transpose(2 * i - 1)
                    if n == 0 and 0 <= i - 2 < NPAIR:
                        x2_transpose(i - 2)
                    if n == 3 and nxt:
                        q_project(i + 1)
                    if 0 <= N - 2 < NQ * NPAIR:
                        probs_transpose(N - 2)
                    if n == 6 and cur:
                        den_transpose(2 * i)
                    if n == 0 and prv:
                        o_project(2 * i - 2)
                    if n == 6 and nxt:
                        v_project(i + 1)
                    if n == (0 if i < 0 else 1) and nxt:
                        k_project(i + 1)
                    if n == 1 and nxt:
                        xn_transpose(i + 1)
                    if n == 3 and prv:
                        o_project(2 * i - 1)
                    if n % 4 in (0, 1) and 0 <= N - 3 < NQ * NPAIR:
                        values(N - 3)
                    if n == 2 and 0 <= i - 2 < NPAIR:
                        route_logits(i - 2)

            pe.wait_ge(s_ch, NPAIR)
            small_free()
            pe.matmul(b_small[:, 0:E], ones_bf[0:S, :], before[:, 2, :],
                      start=True, stop=True).then_inc(s_cnt, 1)
            pe.wait_ge(s_wacc, 1)
            pe.matmul(b_o[:, 0:E], cst[0:S, C_ONE:C_ONE + P], wacc[:, :],
                      start=True, stop=True).then_inc(s_wsum, 1)

            def tile_transpose(t):
                pe.wait_ge(s_in, 16 * (t + 1))
                for c in range(DC):
                    m = pe.transpose(b_xt[:, c * TILE:(c + 1) * TILE], xin[:, c * P:(c + 1) * P], ident)
                m.then_inc(s_xt, 1)

            def three_products(o, pairs_of_parts):
                n = len(pairs_of_parts)
                for k, (lh, ll, rh, rl) in enumerate(pairs_of_parts):
                    pe.matmul(o, lh, rh, start=(k == 0), stop=False)
                    pe.matmul(o, lh, rl, start=False, stop=False)
                    m = pe.matmul(o, ll, rh, start=False, stop=(k == n - 1))
                return m

            def hidden(par, half):
                for which, banks, done in ((0, b_gate, s_gate), (1, b_up, s_up)):
                    wh, wl = wpart(w_hi[par])[which], wpart(w_lo[par])[which]
                    cols = slice(half * HALF, (half + 1) * HALF)
                    three_products(banks[half][:, :], [(x_hi[:, c, :], x_lo[:, c, :], wh[:, c, cols], wl[:, c, cols])
                                                       for c in range(DC)]).then_inc(done, 1)

            def hidden_transpose(t, half):
                pe.wait_ge(s_h, 2 * t + half + 1)
                for f in range(HF):
                    m = pe.transpose(b_ht[half][:, f * TILE:(f + 1) * TILE],
                                     h_sb[:, half, f * P:(f + 1) * P], ident)
                m.then_inc(s_ht, 1)

            def project_down(par, t, half):
                pe.wait_ge(s_hlo, 2 * t + half + 1)
                wh, wl = wpart(w_hi[par])[2], wpart(w_lo[par])[2]
                for f in range(half * HF, (half + 1) * HF):
                    for k, (left, right) in enumerate(((h_hi, wh), (h_hi, wl), (h_lo, wh))):
                        m = pe.matmul(b_y[:, 0:D], left[:, f, :], right[:, f, :],
                                      start=(f == 0 and k == 0), stop=(f == FC - 1 and k == 2))
                m.then_inc(s_down, 1)

            def step(t, par, split_down, next_par, next_split, following):
                hidden_transpose(t, 0)
                hidden(par, 1)
                with ExitStack() as s:
                    if following is not None:
                        s.enter_context(pe.If(following))
                    tile_transpose(t + 1)
                pe.wait_ge(s_wlo, split_down)
                pe.wait_ge(s_y, t + 1)
                project_down(par, t, 0)
                hidden_transpose(t, 1)
                with ExitStack() as s:
                    if following is not None:
                        s.enter_context(pe.If(following))
                    pe.wait_ge(s_wlo, next_split)
                    pe.wait_ge(s_xlo, t + 2)
                    hidden(next_par, 0)
                project_down(par, t, 1)

            pe.wait_ge(s_first, 1)
            tile_transpose(0)
            pe.wait_ge(s_wlo, WCH)
            pe.wait_ge(s_xlo, 1)
            hidden(0, 0)
            with pe.Fori(0, E // 2) as ep:
                for par in range(2):
                    e = 2 * ep + par
                    lo, hi, end, _, following = tiles_of(pe, e)
                    split = pe.to_reg(WCH * (e + 1))
                    split_next = pe.to_reg(WCH * (e + 1) + 2 * CH)
                    with pe.If(end - lo), pe.Fori(lo, end) as t:
                        step(t, par, split, par, split, None)
                    step(end, par, split, 1 - par, split_next, following)

        @block.scalar
        def _(act_e):
            a = act_e
            a.dma_start(attw[:, 1], wT[:, 1]).then_inc(s_wk, 16)
            a.dma_start(attb[:, :, :], bT).then_inc(s_wk, 16)
            a.dma_start(attw[:, 0], wT[:, 0]).then_inc(s_w, 16)
            a.dma_start(biasrow[:, :, :], brow).then_inc(s_w, 16)
            a.dma_start(attw[:, 2:4], wT[:, 2:4]).then_inc(s_w, 16)
            a.dma_start(rw_sb[:, :, :], rwT).then_inc(s_w, 16)
            a.dma_start(rows_sb[:, :], rownum).then_inc(s_w, 16)

            def evac_proj(i, which, ready, done):
                a.wait_ge(ready, i + 1)
                if i >= 1:
                    a.wait_ge(s_krot if which else s_qrot, i)
                for c in range(DC):
                    m = nc.scalar.activation(proj[:, which, 2 * c:2 * c + 2, :],
                                             b_proj[:, c * PT:(c + 1) * PT].rearrange("p (b s) -> p b s", b=2),
                                             ACT.Identity, bias=attb[:, which, c:c + 1])
                m.then_inc(done, 1)

            def den_copy(r):
                a.wait_ge(s_rT, r + 1)
                if r >= 1:
                    a.wait_ge(s_att, r)
                nc.scalar.copy(rdenT[:, :, :].rearrange("p c s -> p (c s)"),
                               b_small[:, 0:DC * S]).then_inc(s_rTc, 1)

            def xn_copy(i):
                a.wait_ge(s_xnT, i + 1)
                if i >= 1:
                    a.wait_ge(s_q, i)
                nc.scalar.copy(xnT[:, :, :].rearrange("p c t -> p (c t)"),
                               b_small[:, 0:DC * PT]).then_inc(s_xnTc, 1)

            def x2_copy(i):
                a.wait_ge(s_x2T, i + 1)
                if i >= 1:
                    a.wait_ge(s_lg, i)
                nc.scalar.copy(xn2T[:, :, :, :].rearrange("p b c s -> p (b c s)"),
                               b_small[:, 0:DC * PT]).then_inc(s_x2Tc, 1)

            a.wait_ge(s_wk, 32)
            for i in range(-1, NPAIR + 2):
                cur, nxt, prv = 0 <= i < NPAIR, i + 1 < NPAIR, 0 <= i - 1 < NPAIR
                for n in range(NQ):
                    N = NQ * i + n
                    if n == 2 and prv:
                        den_copy(2 * i - 1)
                    if n == 6 and cur:
                        den_copy(2 * i)
                    if 0 <= N - 2 < NQ * NPAIR:
                        M = N - 2
                        a.wait_ge(s_pT, M + 1)
                        if M >= 3:
                            a.wait_ge(s_pv, M - 2)
                        nc.scalar.copy(probsT[:, M % 3].rearrange("p h s -> p (h s)"),
                                       b_pt[0:S, 0:QH * S]).then_inc(s_pTc, 1)
                    if n == 0 and 0 <= i - 2 < NPAIR:
                        x2_copy(i - 2)
                    if n == 1 and i == 1:
                        a.dma_start(w_raw[0][:, :], ffw[0]).then_inc(s_raw[0], 16)
                    if cur:
                        a.wait_ge(s_max, N + 1)
                        if N >= 3:
                            a.wait_ge(s_pT, N - 2)
                        r = 2 * i + n // 4
                        if n % 4 == 0 and r >= 2:
                            a.wait_ge(s_rx, r - 1)
                        for h in range(QH):
                            k = n % 4 * QH + h
                            m = nc.scalar.activation(probs[:, N % 3, h, :], b_s[N % 3][0:S, h * S:(h + 1) * S],
                                                     ACT.Exp, bias=negmax[:, N % 4, h:h + 1],
                                                     accum_out=psums[:, r % 2, k:k + 1])
                        m.then_inc(s_p, 1)
                    if n == 1 and nxt:
                        xn_copy(i + 1)
                    if n == (0 if i < 0 else 1) and nxt:
                        evac_proj(i + 1, 1, s_k, s_kc)
                    if n == 2 and nxt:
                        evac_proj(i + 1, 0, s_q, s_qc)

            a.wait_ge(s_dl, 1)
            nc.scalar.activation(etop[:, :, :], delta[:, :, :], ACT.Exp).then_inc(s_et, 1)

            a.wait_ge(s_first, 1)

            def x_high(t):
                a.wait_ge(s_xt, t + 2)
                nc.scalar.copy(x_hi[:, :, :].rearrange("p c t -> p (c t)"), b_xt[:, 0:DC * TILE]).then_inc(s_xhi, 1)

            def silu(t, half):
                a.wait_ge(s_gate, 2 * t + half + 1)
                nc.scalar.activation(act[:, half, :], b_gate[half][:, :], ACT.Silu).then_inc(s_act, 1)

            def hidden_high(t, half):
                a.wait_ge(s_ht, 2 * t + half + 1)
                nc.scalar.copy(h_hi[:, half * HF:(half + 1) * HF, :].rearrange("p f t -> p (f t)"),
                               b_ht[half][:, :]).then_inc(s_hhi, 1)

            def weights_high(par, third, chunk):
                if third is None:
                    return
                col = third * WT + chunk * WC
                nc.scalar.copy(w_hi[1 - par][:, bass.ds(col, WC)], w_raw[par][:, bass.ds(col, WC)]).then_inc(s_whi, 1)

            def step(t, third, par, final=False):
                hidden_high(t, 0)
                weights_high(par, third, 0)
                silu(t, 1)
                weights_high(par, third, 1)
                if not final:
                    x_high(t + 1)
                weights_high(par, third, 2)
                hidden_high(t, 1)
                weights_high(par, third, 3)
                if not final:
                    silu(t + 1, 0)

            def expert(e, par, loaded, reload):
                lo, hi, end, m, _ = tiles_of(a, e)
                if loaded is None:
                    with a.If(end - lo), a.Fori(lo, end) as t:
                        step(t, None, par)
                    step(end, None, par, final=True)
                    return
                left = a.snap((THIRDS - (m - lo)) & 3)
                if reload:
                    a.wait_ge(s_wlo, WCH * (e + 1))
                    a.dma_start(w_raw[1 - par][:, :], ffw[bass.ds(e + 2, 1)].rearrange("e p n -> (e p) n")
                                ).then_inc(s_raw[1 - par], 16)
                with a.If(left), a.Fori(0, left) as third:
                    a.wait_ge(s_down, 2 * lo + 1)
                    a.wait_ge(s_raw[par], loaded)
                    for n in range(CH):
                        weights_high(par, third, n)
                with a.Fori(lo, m) as t:
                    a.wait_ge(s_raw[par], loaded)
                    step(t, nc.s_assert_within((t - lo + left) & 3, 0, THIRDS - 1), par)
                with a.If(hi - m), a.Fori(m, hi) as t:
                    step(t, None, par)

            x_high(0)
            silu(0, 0)
            with a.Fori(0, E // 2 - 1) as ep:
                for par in range(2):
                    expert(2 * ep + par, par, a.to_reg(16 * (ep + 2 - par)), True)
            expert(E - 2, 0, 16 * (E // 2 + 1), False)
            expert(E - 1, 1, None, False)

        @block.vector
        def _(v):
            V = nc.vector
            links = [0]

            def link(ins):
                links[0] += 1
                ins.then_inc(dve, 1)
                v.wait_ge(dve, links[0])

            def bc(ap, shape):
                return ap.to_broadcast(shape)

            link(V.memset(before[:, :, :], 0.0))

            def norm_stats(src, st, m, done):
                for b in range(2):
                    V.bn_stats(st[:, b, :], src[:, b, :]).then_inc(dve, 1)
                    links[0] += 1
                v.wait_ge(dve, links[0])
                for b in range(2):
                    ins = V.bn_aggr(m[:, b, :], st[:, b, :])
                ins.then_inc(done, 1)

            def xn_stats(i):
                v.wait_ge(s_x[min(i, 2)], 16)
                norm_stats(x_all[:, 2 * i:2 * i + 2, :], stats, mv, s_var)

            def xn_write(i):
                v.wait_ge(s_rstd, i + 1)
                if i:
                    v.wait_ge(s_xnT, i)
                for b in range(2):
                    ins = V.tensor_scalar(xn[:, b, :], x_all[:, 2 * i + b, :], mv[:, b, 0:1], rstd[:, b:b + 1],
                                          ALU.subtract, ALU.mult)
                ins.then_inc(s_xn, 1)

            rope = cst[:, C_ROPE:C_ROPE + 4 * S].rearrange("p (t s) -> p t s", t=4)

            def rotate(i, which, ready, o, done):
                v.wait_ge(ready, i + 1)
                src, sw = proj[:, which], swap[:, which]
                link(V.stream_shuffle(sw, src, [p ^ (DH // 2) for p in range(32)]))
                V.tensor_tensor(src, src, bc(rope[:, 2 * which:2 * which + 1, :], [P, 2 * DC, S]), ALU.mult)
                link(V.tensor_tensor(sw, sw, bc(rope[:, 2 * which + 1:2 * which + 2, :], [P, 2 * DC, S]), ALU.mult))
                V.tensor_tensor(o, src, sw, ALU.add).then_inc(done, 1)

            def k_rotate(i):
                if i:
                    for q in s_kblk:
                        v.wait_ge(q, 16 * HC * i)
                rotate(i, 1, s_kc, krot[:, :, :], s_krot)

            def q_rotate(i):
                if i >= 2:
                    v.wait_ge(s_s, NQ * (i - 1))
                rotate(i, 0, s_qc, qrot[:, i % 2], s_qrot)

            def v_write(i):
                v.wait_ge(s_v, i + 1)
                if i >= 2:
                    v.wait_ge(s_pv, NQ * (i - 1))
                V.tensor_tensor(v_sb[:, i % 2], b_proj[0:S, 0:2 * D].rearrange("p (b d) -> p b d", b=2),
                                bc(biasrow[:, 0:1, :], [S, 2, D]), ALU.add).then_inc(s_vc, 1)

            def den(r):
                v.wait_ge(s_p, 4 * r + 4)
                link(V.reciprocal(rden[:, r % 2, :], psums[:, r % 2, :]))
                if r:
                    v.wait_ge(s_rT, r)
                V.tensor_copy(rdenx[:, :, :], bc(rden[:, r % 2, :].unsqueeze(2), [S, H, DH])).then_inc(s_rx, 1)

            def attend(r):
                b = r % 2
                v.wait_ge(s_pv, 4 * r + 4)
                v.wait_ge(s_rTc, r + 1)
                pv = b_pv[:, 0:DC * PT].rearrange("p (c h s) -> p c h s", c=DC, h=2)
                V.scalar_tensor_tensor(out=ev0[:, :, :], in0=pv[:, :, 0, :], scalar=cst[:, C_PAR:C_PAR + 1],
                                       in1=rdenT[:, :, :], op0=ALU.mult, op1=ALU.mult)
                link(V.scalar_tensor_tensor(out=ev1[:, :, :], in0=pv[:, :, 1, :],
                                            scalar=cst[:, C_PAR + 1:C_PAR + 2],
                                            in1=rdenT[:, :, :], op0=ALU.mult, op1=ALU.mult))
                if r >= 2:
                    v.wait_ge(s_o, r - 1)
                V.tensor_tensor(att[:, b], ev0[:, :, :], ev1[:, :, :], ALU.add).then_inc(s_att, 1)

            def residual(i):
                v.wait_ge(s_o, 2 * i + 2)
                xs = x_all[:, 2 * i:2 * i + 2, :]
                v.wait_ge(s_xob, i + 1)
                ins = V.tensor_tensor(xs, b_o[0:S, 0:2 * D].rearrange("p (b d) -> p b d", b=2), xs, ALU.add)
                ins.then_inc(s_x2, 1)
                v.wait_ge(s_x2, i + 1)
                norm_stats(xs, stats2, mv2, s_var2)

            def rows_write(i):
                v.wait_ge(s_rstd2, i + 1)
                if i >= 2:
                    v.wait_ge(s_scat[i % 2], 16 * TOPK * 2 * (i // 2))
                for b in range(2):
                    V.tensor_copy(xrow[:, i % 2, b, D:RW].bitcast(I32), rows_sb[0:S, 2 * i + b:2 * i + b + 1])
                    ins = V.tensor_scalar(xrow[:, i % 2, b, 0:D], x_all[:, 2 * i + b, :], mv2[:, b, 0:1],
                                          rstd2[:, b:b + 1], ALU.subtract, ALU.mult)
                ins.then_inc(s_xr, 1)

            def choose(i):
                v.wait_ge(s_lg, i + 1)
                V.tensor_copy(logits[:, :, :].rearrange("p b e -> p (b e)"), b_small[0:S, 0:2 * E]).then_inc(s_lgc, 1)
                v.wait_ge(s_lgc, i + 1)
                for b in range(2):
                    V.max(top[:, i, b, :], logits[:, b, :]).then_inc(dve, 1)
                    links[0] += 1
                v.wait_ge(dve, links[0])
                for b in range(2):
                    V.max_index(topi[:, b, :], top[:, i, b, :], logits[:, b, :]).then_inc(dve, 1)
                    links[0] += 1

            def choose_masks(i):
                v.wait_ge(dve, links[0])
                link(V.tensor_copy(choice[:, :, :].rearrange("p k b -> p b k"), topi[:, :, 0:TOPK]))
                m = sel[:, i]
                V.tensor_copy(before[:, 0, :], before[:, 2, :])
                link(V.tensor_tensor(m, bc(cst[0:S, C_EXP:C_EXP + E].unsqueeze(1), [S, 4, E]),
                                     bc(choice[:, :, :].rearrange("p k b -> p (k b)").unsqueeze(2), [S, 4, E]),
                                     ALU.is_equal))

            def choose_counts(i):
                m = sel[:, i]
                link(V.tensor_tensor(chosen[:, :, :], m[:, 0:2, :], m[:, 2:4, :], ALU.add))
                link(V.tensor_tensor(before[:, 1, :], before[:, 0, :], chosen[:, 0, :], ALU.add))
                V.tensor_tensor(before[:, 2, :], before[:, 1, :], chosen[:, 1, :], ALU.add).then_inc(s_ch, 1)

            def places(i):
                v.wait_ge(s_rk, i + 1)
                V.tensor_tensor(place[:, :, :], b_small[0:S, 0:2 * E].rearrange("p (b e) -> p b e", b=2),
                                bc(cst[0:S, C_BASE:C_BASE + E].unsqueeze(1), [S, 2, E]), ALU.add
                                ).then_inc(s_rkc, 1)
                v.wait_ge(s_rkc, i + 1)
                m = sel[:, i]
                for k in range(TOPK):
                    ins = V.tensor_tensor(placed[:, 2 * k:2 * k + 2, :], m[:, 2 * k:2 * k + 2, :], place[:, :, :], ALU.mult)
                link(ins)
                link(V.tensor_reduce(dest[:, :], placed[:, :, :], AX.X, ALU.add))
                if i >= 2:
                    v.wait_ge(s_scat[i % 2], 16 * TOPK * 2 * (i // 2))
                V.tensor_copy(desti[:, i % 2, :], dest[:, :]).then_inc(s_dest, 1)

            for n, free in enumerate((s_xt, s_id, s_down, s_idnow, s_scaled, s_scaled)):
                V.memset(credit[:, n:n + 1], 0.0).then_inc(free, 1)
            xn_stats(0)
            v.wait_ge(s_cst, 16)
            V.tensor_copy(ident_bf[:, :], cst[:, C_ID:C_ID + P]).then_inc(s_setup, 1)
            V.tensor_copy(tri_bf[:, :], cst[:, C_TRI:C_TRI + P]).then_inc(s_setup, 1)
            V.tensor_copy(ones_bf[:, :], cst[:, C_ONE:C_ONE + P]).then_inc(s_setup, 1)
            V.tensor_copy(mask_bf[:, :, :],
                          bc(cst[:, C_MASK:C_MASK + S].unsqueeze(1), [P, QH, S])).then_inc(s_setup, 1)
            for i in range(-1, NPAIR + 2):
                cur, nxt, prv, old = 0 <= i < NPAIR, i + 1 < NPAIR, 0 <= i - 1 < NPAIR, 0 <= i - 2
                for n in range(NQ):
                    N = NQ * i + n
                    if n == 3 and 0 <= i - 2 < NPAIR:
                        choose_masks(i - 2)
                    if cur:
                        v.wait_ge(s_s, N + 1)
                        if N >= 4:
                            v.wait_ge(s_p, N - 3)
                        V.tensor_reduce(negmax[:, N % 4, :],
                                        b_s[N % 3][0:S, 0:QH * S].rearrange("p (h s) -> p h s", h=QH),
                                        AX.X, ALU.max, negate=True).then_inc(s_max, 1)
                    if n == 0 and nxt:
                        xn_write(i + 1)
                    if n == 1 and prv:
                        den(2 * i - 1)
                    if n == 2 and prv:
                        attend(2 * i - 1)
                    if n == (0 if i < 0 else 2) and nxt:
                        k_rotate(i + 1)
                    if n == 2 and 0 <= i - 2 < NPAIR:
                        choose(i - 2)
                    if n == 3 and 0 <= i - 2 < NPAIR:
                        choose_counts(i - 2)
                    if n == 4 and prv:
                        residual(i - 1)
                    if n == 5 and cur:
                        den(2 * i)
                    if n == 5 and 0 <= i - 2 < NPAIR:
                        places(i - 2)
                    if n == 5 and nxt:
                        q_rotate(i + 1)
                    if n == 6 and cur:
                        attend(2 * i)
                    if n == 6 and prv:
                        rows_write(i - 1)
                    if n == 7 and nxt:
                        if i < 0:
                            v.wait_ge(s_w, 16 * 5)
                        v_write(i + 1)
                    if n == 7 and i + 2 < NPAIR:
                        xn_stats(i + 2)

            V.tensor_tensor(delta[:, :, :].rearrange("p k t -> p t k"),
                            top[:, :, :, 0:TOPK].rearrange("p i b k -> p (i b) k"),
                            bc(top[:, :, :, 0:1].rearrange("p i b k -> p (i b) k"), [S, B, TOPK]),
                            ALU.subtract).then_inc(s_dl, 1)
            v.wait_ge(s_cnt, 1)
            link(V.tensor_copy(cnt[:, :], b_small[:, 0:E]))
            V.tensor_tensor(taili[:, :], cnt[:, :], cst[:, C_TAIL:C_TAIL + E], ALU.add).then_inc(s_tail, 1)
            link(V.tensor_tensor(over[:, :, :], bc(cnt[0:1, :].unsqueeze(2), [1, E, MAXT - 1]),
                                 cst[0:1, C_THR:C_LT].rearrange("p (e j) -> p e j", e=E), ALU.is_gt))
            link(V.tensor_reduce(ntile[:, :], over[:, :, :], AX.X, ALU.add))
            link(V.tensor_scalar(ntile1[:, :], ntile[:, :], 1.0, None, ALU.add))
            link(V.tensor_tensor(upto[:, :, :], bc(ntile1[:, :].unsqueeze(1), [1, E + 1, E]),
                                 cst[0:1, C_LT:C_ALL].rearrange("p (j e) -> p j e", e=E), ALU.mult))
            link(V.tensor_reduce(first_f[:, :], upto[:, :, :], AX.X, ALU.add))
            V.tensor_copy(first[:, :], first_f[:, :])
            V.tensor_scalar(more[:, :], cst[0:1, C_EXP:C_EXP + E], float(E - 1), None, ALU.is_lt)
            link(V.tensor_scalar(nsplit[:, :], ntile1[:, :], float(THIRDS), None, ALU.min))
            V.scalar_tensor_tensor(out=plan_a[:, :], in0=first_f[:, 1:E + 1], scalar=float(1 << FIELD),
                                   in1=first_f[:, 0:E], op0=ALU.mult, op1=ALU.add)
            link(V.tensor_tensor(mid[:, :], first_f[:, 0:E], nsplit[:, :], ALU.add))
            link(V.scalar_tensor_tensor(out=plan_b[:, :], in0=mid[:, :], scalar=float(1 << 2 * FIELD),
                                        in1=plan_a[:, :], op0=ALU.mult, op1=ALU.add))
            V.scalar_tensor_tensor(out=plan[:, :], in0=more[:, :], scalar=float(1 << 3 * FIELD),
                                   in1=plan_b[:, :], op0=ALU.mult, op1=ALU.add).then_inc(s_first, 1)
            link(V.tensor_scalar(cnt1[:, :], cnt[:, :], 1.0, None, ALU.max))
            link(V.reciprocal(crec[:, :], cnt1[:, :]))
            v.wait_ge(s_et, 1)
            link(V.tensor_tensor(esum[:, :], etop[:, 0, :], etop[:, 1, :], ALU.add))
            link(V.reciprocal(erec[:, :], esum[:, :]))
            link(V.tensor_tensor(wtop[:, :, :], etop[:, :, :], bc(erec[:, :].unsqueeze(1), [S, TOPK, B]), ALU.mult))
            for k in range(TOPK):
                ins = V.tensor_tensor(wsel[:, :, 2 * k:2 * k + 2, :], sel[:, :, 2 * k:2 * k + 2, :],
                                      bc(wtop[:, k, :].rearrange("p (i b) -> p i b", b=2).unsqueeze(3),
                                         [S, NPAIR, 2, E]), ALU.mult)
            link(ins)
            V.tensor_reduce(wacc[:, :], wsel[:, :, :, :].rearrange("p i k e -> p e (i k)"), AX.X,
                            ALU.add).then_inc(s_wacc, 1)
            v.wait_ge(s_wsum, 1)
            V.tensor_tensor(meanw[:, :], b_o[:, 0:E], crec[:, :], ALU.mult).then_inc(s_mean, 1)

            v.wait_ge(s_first, 1)

            def x_low(t):
                v.wait_ge(s_xhi, t + 1)
                V.tensor_tensor(x_lo[:, :, :].rearrange("p c t -> p (c t)"), b_xt[:, 0:DC * TILE],
                                x_hi[:, :, :].rearrange("p c t -> p (c t)"), ALU.subtract).then_inc(s_xlo, 1)

            def take_ids(t, column):
                v.wait_ge(s_in, 16 * (t + 1))
                V.tensor_copy(idnext[:, column], xin[:, D:RW].bitcast(I32)).then_inc(s_id, 1)

            def gated(t, half):
                v.wait_ge(s_up, 2 * t + half + 1)
                v.wait_ge(s_act, 2 * t + half + 1)
                V.tensor_tensor(h_sb[:, half, :], b_up[half][:, :], act[:, half, :], ALU.mult).then_inc(s_h, 1)

            def hidden_low(t, half):
                v.wait_ge(s_hhi, 2 * t + half + 1)
                rows = slice(half * HF, (half + 1) * HF)
                V.tensor_tensor(h_lo[:, rows, :].rearrange("p f t -> p (f t)"), b_ht[half][:, :],
                                h_hi[:, rows, :].rearrange("p f t -> p (f t)"), ALU.subtract).then_inc(s_hlo, 1)

            def take_output(t):
                v.wait_ge(s_down, 2 * t + 1)
                v.wait_ge(s_scaled, t + 1)
                V.tensor_copy(y_raw[:, :], b_y[:, 0:D]).then_inc(s_y, 1)

            def weights_low(e, par, third, chunk):
                if third is None:
                    return
                col = third * WT + chunk * WC
                v.wait_ge(s_whi, WCH * e + CH * third + (chunk + 1))
                V.tensor_tensor(w_lo[1 - par][:, bass.ds(col, WC)], w_raw[par][:, bass.ds(col, WC)],
                                w_hi[1 - par][:, bass.ds(col, WC)], ALU.subtract).then_inc(s_wlo, 1)

            def step(e, t, third, par, final=False):
                hidden_low(t, 0)
                take_output(t)
                weights_low(e, par, third, 0)
                gated(t, 1)
                weights_low(e, par, third, 1)
                if not final:
                    x_low(t + 1)
                weights_low(e, par, third, 2)
                hidden_low(t, 1)
                if not final:
                    v.wait_ge(s_idnow, t + 1)
                    take_ids(t + 1, bass.ds((t + 1) & 1, 1))
                weights_low(e, par, third, 3)
                if not final:
                    gated(t + 1, 0)

            def expert(e, par, split):
                lo, hi, end, m, _ = tiles_of(v, e)
                if not split:
                    with v.If(end - lo), v.Fori(lo, end) as t:
                        step(e, t, None, par)
                    step(e, end, None, par, final=True)
                    take_output(hi)
                    return
                left = v.snap((THIRDS - (m - lo)) & 3)
                with v.If(left), v.Fori(0, left) as third:
                    for n in range(CH):
                        weights_low(e, par, third, n)
                with v.Fori(lo, m) as t:
                    step(e, t, nc.s_assert_within((t - lo + left) & 3, 0, THIRDS - 1), par)
                with v.If(hi - m), v.Fori(m, hi) as t:
                    step(e, t, None, par)

            x_low(0)
            take_ids(0, slice(0, 1))
            gated(0, 0)
            with v.Fori(0, E // 2 - 1) as ep:
                for par in range(2):
                    expert(2 * ep + par, par, True)
            expert(E - 2, 0, True)
            expert(E - 1, 1, False)

        @block.gpsimd
        def _(g):
            G = nc.gpsimd
            G.memset(tailrow[:, :], 0.0).then_inc(s_zero, 1)
            G.memset(eps_exp[:, :], -0.5).then_inc(s_zero, 1)
            G.memset(kblk[:, :, :, :, :].rearrange("p a c h t -> p (a c h t)"), 0.0).then_inc(s_zero, 1)
            ps = [0]

            def inverse_deviation(i, var, m, v_e, o, done, used):
                g.wait_ge(var, i + 1)
                if i:
                    g.wait_ge(used, i)
                G.tensor_scalar(v_e[:, :], m[:, :, 1], EPS, None, ALU.add).then_inc(pool_self, 1)
                ps[0] += 1
                g.wait_ge(pool_self, ps[0])
                G.tensor_tensor(o[:, :], v_e[:, :], eps_exp[0:S, :], ALU.pow).then_inc(done, 1)

            def scatter(i):
                g.wait_ge(s_dest, i + 1)
                for k in range(TOPK):
                    for b in range(2):
                        c = 2 * k + b
                        G.indirect_dma_start(slots, bass.IndirectOffsetOnAxis(desti[:, i % 2, c:c + 1], 0),
                                             xrow[:, i % 2, b, :], None).then_inc(s_scat[i % 2], 16)

            g.wait_ge(s_zero, 3)
            for i in range(-1, NPAIR + 2):
                if i + 1 < NPAIR:
                    if i == -1:
                        inverse_deviation(0, s_var, mv, ve, rstd, s_rstd, s_xn)
                    g.wait_ge(s_xn, i + 2)
                    if i < 0:
                        g.wait_ge(s_w, 16 * 5)
                    xs = x_all[:, 2 * i + 2:2 * i + 4, :]
                    G.tensor_tensor(xs, xs, biasrow[:, 1:2, :].to_broadcast([S, 2, D]), ALU.add).then_inc(s_xob, 1)
                if 0 <= i - 1 < NPAIR:
                    inverse_deviation(i - 1, s_var2, mv2, ve2, rstd2, s_rstd2, s_xr)
                if 0 <= i - 2 < NPAIR:
                    scatter(i - 2)
                if i + 2 < NPAIR:
                    inverse_deviation(i + 2, s_var, mv, ve, rstd, s_rstd, s_xn)
                if 1 <= i < 7:
                    g.wait_ge(s_raw[0], 16)
                    for n in range((i - 1) * WCH // 6, i * WCH // 6):
                        cols = slice(n * WC, (n + 1) * WC)
                        G.tensor_copy(w_hi[0][:, cols], w_raw[0][:, cols]).then_inc(pool_self, 1)
                        ps[0] += 1
                        g.wait_ge(pool_self, ps[0])
                        G.tensor_tensor(w_lo[0][:, cols], w_raw[0][:, cols], w_hi[0][:, cols],
                                        ALU.subtract).then_inc(s_wlo, 1)

            g.wait_ge(s_pad, 16)
            G.tensor_copy(tailrow[:, D:RW].bitcast(I32), rows_sb[:, B:B + 1]).then_inc(pool_self, 1)
            ps[0] += 1
            g.wait_ge(pool_self, ps[0])
            g.wait_ge(s_tail, 1)
            for e in range(E):
                G.indirect_dma_start(slots, bass.IndirectOffsetOnAxis(taili[:, e:e + 1], 0),
                                     tailrow[:, :], None).then_inc(s_tails[e], 16)

            g.wait_ge(s_first, 1)
            g.wait_ge(s_pad, 16)
            g.wait_ge(s_out, 16 * NPAIR)
            g.wait_ge(s_mean, 1)
            with g.Fori(0, E) as e:
                lo, hi, _, _, _ = tiles_of(g, e)
                copied = g.to_reg(e + 2)
                G.tensor_copy(mean1[:, :], meanw[:, bass.ds(e, 1)]).then_inc(s_mean, 1)
                g.wait_ge(s_first, 1)
                g.wait_ge(s_mean, copied)
                with g.Fori(lo, hi) as t:
                    taken, scaled, added = g.to_reg(t + 2), g.to_reg(t + 3), g.to_reg(16 * (t + 1))
                    g.wait_ge(s_first, 1)
                    g.wait_ge(s_id, taken)
                    G.tensor_copy(idnow[:, :], idnext[:, bass.ds(t & 1, 1)]).then_inc(s_idnow, 1)
                    g.wait_ge(s_first, 1)
                    g.wait_ge(s_y, taken)
                    G.tensor_scalar(y_sb[:, :], y_raw[:, :], mean1[:, 0:1], None,
                                    ALU.mult).then_inc(s_scaled, 1)
                    g.wait_ge(s_first, 1)
                    g.wait_ge(s_scaled, scaled)
                    g.wait_ge(s_idnow, taken)
                    G.indirect_dma_start(out, bass.IndirectOffsetOnAxis(idnow[:, 0:1], 0), y_sb[:, :], None,
                                         bounds_check=TOK + P - 1, oob_is_err=True,
                                         compute_op=ALU.add).then_inc(s_add, 16)
                    g.wait_ge(s_first, 1)
                    g.wait_ge(s_add, added)


def kernel(**inputs):
    import concourse.bacc as _bacc
    from concourse.bass_utils import run_bass_kernel_spmd as _run

    def arr(n):
        return np.asarray(inputs[n])

    def chunks(w):
        t = np.swapaxes(w, -1, -2)
        t = t.reshape(t.shape[:-2] + (t.shape[-2] // P, P, t.shape[-1]))
        return np.ascontiguousarray(np.swapaxes(t, -3, -2))

    x = np.ascontiguousarray(arr("x"))
    ctxT = np.ascontiguousarray(arr("ctx_1024")[:, :S].reshape(TOK, DC, P).transpose(2, 1, 0))
    wT = np.stack([chunks(arr(f"L0_xattn_{n}_w")) for n in "qkvo"], 1)
    bT = np.stack([arr(f"L0_xattn_{n}_b").reshape(DC, P).T for n in "qk"], 1)
    brow = np.ascontiguousarray(np.broadcast_to(np.stack([arr(f"L0_xattn_{n}_b") for n in "vo"]), (S, 2, D)))
    rwT = chunks(arr("L0_ffn_router_w"))
    ffw = np.concatenate([chunks(arr(f"L0_ffn_{n}_w")).reshape(E, P, -1) for n in ("gate", "up", "down")], -1)
    consts, rownum = shape_constants()
    host = {"x": x, "ctxT": ctxT, "wT": wT, "bT": np.ascontiguousarray(bT), "brow": brow, "rwT": rwT,
            "ffw": ffw, "consts": consts, "rownum": rownum}

    nc = _bacc.Bacc("TRN2", target_bir_lowering=False, num_devices=1)
    args = [nc.dram_tensor(f"in_{k}", a.shape, mybir.dt.from_np(a.dtype), kind="ExternalInput").ap()
            for k, a in host.items()]
    out = nc.dram_tensor("out_0", (TOK + P, D), F32, kind="ExternalOutput").ap()
    build(nc, *args, out)
    r = _run(nc, [{f"in_{k}": a for k, a in host.items()}], core_ids=[0])
    return r.results[0]["out_0"][:TOK].reshape(B, S, D)
```
